# Optimizing a Trainium2 kernel written in Bass

```python
import numpy as np
import jax
import jax.numpy as jnp

def _softmax(x, axis=-1):
    return jax.nn.softmax(x, axis=axis)

def _gelu(x):
    return jax.nn.gelu(x, approximate=True)

def _silu(x):
    return jax.nn.silu(x)

def _sigmoid(x):
    return jax.nn.sigmoid(x)

def _layernorm(x, axis=-1, eps=1e-05):
    m = jnp.mean(x, axis=axis, keepdims=True)
    v = jnp.var(x, axis=axis, keepdims=True)
    return (x - m) / jnp.sqrt(v + eps)

def _scatter_add(tgt, idx, src, axis=0):
    return tgt.at[idx].add(src)

def _segment_sum(src, seg, n):
    return jax.ops.segment_sum(src, seg, n)
kernel_name = 'mk_seq_postln_d1_jaxref_r4_91b065'

def setup_inputs(seed: int=0):
    np.random.seed(seed)
    _w = jnp.asarray

    def _L0_attn_setup():
        import jax, jax.numpy as jnp
        import numpy as np
        EMBED_DIM = 256
        NUM_HEADS = 16
        HEAD_DIM = EMBED_DIM // NUM_HEADS

        def _feature_map(x):
            return jax.nn.elu(x) + 1.0

        def _split_heads(x, bsz, seq_len):
            return x.reshape(bsz, seq_len, NUM_HEADS, HEAD_DIM).transpose(0, 2, 1, 3)
        key = jax.random.key(seed)
        ks = jax.random.split(key, 9)
        s = 0.02
        E = EMBED_DIM
        return {'hidden_states': jax.random.normal(ks[0], (4, 1024, E), dtype=jnp.float32), 'Wq': jax.random.normal(ks[1], (E, E), dtype=jnp.float32) * s, 'bq': jnp.zeros((E,), dtype=jnp.float32), 'Wk': jax.random.normal(ks[2], (E, E), dtype=jnp.float32) * s, 'bk': jnp.zeros((E,), dtype=jnp.float32), 'Wv': jax.random.normal(ks[3], (E, E), dtype=jnp.float32) * s, 'bv': jnp.zeros((E,), dtype=jnp.float32), 'Wo': jax.random.normal(ks[4], (E, E), dtype=jnp.float32) * s, 'bo': jnp.zeros((E,), dtype=jnp.float32)}
    _L0_attn_in = _L0_attn_setup()

    def _L0_ffn_setup():
        import jax, jax.numpy as jnp
        import numpy as np
        LN_EPS = 1e-05

        def layer_norm(x, g, b):
            mu = jnp.mean(x, axis=-1, keepdims=True)
            var = jnp.mean(jnp.square(x - mu), axis=-1, keepdims=True)
            return (x - mu) * jax.lax.rsqrt(var + LN_EPS) * g + b

        def ternary_quant(w):
            scale = 1.0 / jnp.clip(jnp.mean(jnp.abs(w)), 1e-05)
            wq = jnp.clip(jnp.round(w * scale), -1.0, 1.0) / scale
            return w + jax.lax.stop_gradient(wq - w)
        key = jax.random.key(seed)
        ks = jax.random.split(key, 3)
        dim, hidden = (256, 1024)
        B, S = (8, 256)
        x = jax.random.normal(ks[0], (B, S, dim), dtype=jnp.float32)
        w1 = jax.random.normal(ks[1], (hidden, dim), dtype=jnp.float32) * 0.02
        w2 = jax.random.normal(ks[2], (dim, hidden), dtype=jnp.float32) * 0.02
        return {'x': x, 'ln1_g': jnp.ones((dim,), jnp.float32), 'ln1_b': jnp.zeros((dim,), jnp.float32), 'w1': w1, 'b1': jnp.zeros((hidden,), jnp.float32), 'ln2_g': jnp.ones((hidden,), jnp.float32), 'ln2_b': jnp.zeros((hidden,), jnp.float32), 'w2': w2, 'b2': jnp.zeros((dim,), jnp.float32)}
    _L0_ffn_in = _L0_ffn_setup()
    _d = {'L0_attn_hidden_states': _L0_attn_in['hidden_states'], 'L0_attn_Wq': _L0_attn_in['Wq'], 'L0_attn_bq': _L0_attn_in['bq'], 'L0_attn_Wk': _L0_attn_in['Wk'], 'L0_attn_bk': _L0_attn_in['bk'], 'L0_attn_Wv': _L0_attn_in['Wv'], 'L0_attn_bv': _L0_attn_in['bv'], 'L0_attn_Wo': _L0_attn_in['Wo'], 'L0_attn_bo': _L0_attn_in['bo'], 'L0_ffn_ln1_g': _L0_ffn_in['ln1_g'], 'L0_ffn_ln1_b': _L0_ffn_in['ln1_b'], 'L0_ffn_w1': _L0_ffn_in['w1'], 'L0_ffn_b1': _L0_ffn_in['b1'], 'L0_ffn_ln2_g': _L0_ffn_in['ln2_g'], 'L0_ffn_ln2_b': _L0_ffn_in['ln2_b'], 'L0_ffn_w2': _L0_ffn_in['w2'], 'L0_ffn_b2': _L0_ffn_in['b2']}
    _x0 = _d['L0_attn_hidden_states']
    _d['L0_attn_hidden_states'] = jax.random.normal(jax.random.fold_in(jax.random.key(seed), 1), (8, 1024, 256), dtype=_x0.dtype)
    del _x0
    return _d

def reference(L0_attn_hidden_states, L0_attn_Wq, L0_attn_bq, L0_attn_Wk, L0_attn_bk, L0_attn_Wv, L0_attn_bv, L0_attn_Wo, L0_attn_bo, L0_ffn_ln1_g, L0_ffn_ln1_b, L0_ffn_w1, L0_ffn_b1, L0_ffn_ln2_g, L0_ffn_ln2_b, L0_ffn_w2, L0_ffn_b2):

    def _L0_attn_ref(hidden_states, Wq, bq, Wk, bk, Wv, bv, Wo, bo):
        import jax, jax.numpy as jnp
        import numpy as np
        EMBED_DIM = 256
        NUM_HEADS = 16
        HEAD_DIM = EMBED_DIM // NUM_HEADS

        def _feature_map(x):
            return jax.nn.elu(x) + 1.0

        def _split_heads(x, bsz, seq_len):
            return x.reshape(bsz, seq_len, NUM_HEADS, HEAD_DIM).transpose(0, 2, 1, 3)
        bsz, tgt_len, _ = hidden_states.shape
        q = _feature_map(hidden_states @ Wq.T + bq)
        k = _feature_map(hidden_states @ Wk.T + bk)
        v = hidden_states @ Wv.T + bv
        q = _split_heads(q, bsz, tgt_len)
        k = _split_heads(k, bsz, tgt_len)
        v = _split_heads(v, bsz, tgt_len)
        KV = jnp.einsum('bhsd,bhsm->bhmd', k, v)
        Z = 1.0 / (jnp.einsum('bhsd,bhd->bhs', q, k.sum(axis=2)) + 1e-06)
        attn = jnp.einsum('bhsd,bhmd,bhs->bshm', q, KV, Z)
        attn = attn.reshape(bsz, tgt_len, EMBED_DIM)
        return attn @ Wo.T + bo

    def _L0_ffn_ref(x, ln1_g, ln1_b, w1, b1, ln2_g, ln2_b, w2, b2):
        import jax, jax.numpy as jnp
        import numpy as np
        LN_EPS = 1e-05

        def layer_norm(x, g, b):
            mu = jnp.mean(x, axis=-1, keepdims=True)
            var = jnp.mean(jnp.square(x - mu), axis=-1, keepdims=True)
            return (x - mu) * jax.lax.rsqrt(var + LN_EPS) * g + b

        def ternary_quant(w):
            scale = 1.0 / jnp.clip(jnp.mean(jnp.abs(w)), 1e-05)
            wq = jnp.clip(jnp.round(w * scale), -1.0, 1.0) / scale
            return w + jax.lax.stop_gradient(wq - w)
        h = layer_norm(x, ln1_g, ln1_b)
        h = jnp.einsum('bsd,hd->bsh', h, ternary_quant(w1)) + b1
        h = jax.nn.gelu(h, approximate=False)
        h = layer_norm(h, ln2_g, ln2_b)
        out = jnp.einsum('bsh,dh->bsd', h, ternary_quant(w2)) + b2
        return out
    x = L0_attn_hidden_states
    x = _layernorm(x + _L0_attn_ref(x, L0_attn_Wq, L0_attn_bq, L0_attn_Wk, L0_attn_bk, L0_attn_Wv, L0_attn_bv, L0_attn_Wo, L0_attn_bo), axis=-1)
    x = _layernorm(x + _L0_ffn_ref(x, L0_ffn_ln1_g, L0_ffn_ln1_b, L0_ffn_w1, L0_ffn_b1, L0_ffn_ln2_g, L0_ffn_ln2_b, L0_ffn_w2, L0_ffn_b2), axis=-1)
    return x

_drawn_inputs = setup_inputs


def setup_inputs(seed=0):
    import zlib

    import numpy as np

    out = dict(_drawn_inputs(seed))
    spreads = {'L0_attn_bq': (0.0, 2.0),
     'L0_attn_bk': (0.0, 2.0),
     'L0_attn_bv': (0.0, 0.267),
     'L0_attn_bo': (0.0, 0.1),
     'L0_ffn_ln1_g': (1.0, 0.2),
     'L0_ffn_ln1_b': (0.0, 0.1),
     'L0_ffn_b1': (0.0, 0.1),
     'L0_ffn_ln2_g': (1.0, 0.2),
     'L0_ffn_ln2_b': (0.0, 0.1),
     'L0_ffn_b2': (0.0, 0.1)}
    factors = {'L0_attn_Wq': 32.133, 'L0_attn_Wk': 22.407, 'L0_attn_Wv': 8.0}
    for name, (base, spread) in spreads.items():
        noise = np.random.default_rng([zlib.crc32(name.encode()), seed]).standard_normal(out[name].shape)
        drawn = base * np.exp(spread * noise) if base else spread * noise
        out[name] = jnp.asarray(drawn.astype(out[name].dtype))
    for name, factor in factors.items():
        out[name] = (out[name] * factor).astype(out[name].dtype)
    return out
```

```python
from contextlib import ExitStack

import concourse.bass as bass
from concourse import mybir

F32 = mybir.dt.float32
F32R = mybir.dt.float32r
ALU = mybir.AluOpType
ACT = mybir.ActivationFunctionType
AX = mybir.AxisListType

P = 128
ATTN_EPS = 1e-6
LN_EPS = 1e-5
SCALE_FLOOR = 1e-5


class Uses:

    def __init__(self, first, bank, banks):
        self.first, self.bank, self.banks, self.k = first, bank, banks, 0

    def take(self):
        k = self.k
        self.k += 1
        return self.first + k, (self.bank + k) % self.banks


class Half:

    def __init__(self, n, lap=0):
        self.n, self.lap, self.par = n, lap, n % 2

    def at(self, per_half, k=0):
        return per_half * self.n + k + 2 * per_half * self.lap

    def ahead(self, d):
        return Half(self.n + d, self.lap)


def block_kernel(nc, x, Wq, bq, Wk, bk, Wv, bv, Wo, bo, ln1_g, ln1_b, w1, b1, ln2_g, ln2_b, w2, b2, out):
    B, S, E = x.shape
    HID = w1.shape[0]
    HEADS = 16
    HD = E // HEADS
    TOK = 512
    NH = B * S // TOK
    NT = TOK // P
    EC = E // P
    HC = HID // P
    HB = P // HD
    AW = P + HB
    VW = P + 4
    assert S == 2 * TOK and EC == 2 and HC == 8 and NT == 4 and NH % 2 == 0 and NH >= 6

    T_PRO, M_PRO, F_PRO = 21, 2 * NT, 2 * EC
    T_AT, M_AT, F_AT = [T_PRO], [M_PRO], [F_PRO]
    for n in range(NH + 1):
        near, late = n < NH - 2, n >= 1
        T_AT.append(T_AT[n] + EC * near + NT + NT * late + 2 * EC * (n < NH) + NT)
        M_AT.append(M_AT[n] + NT * near + NT + NT * late)
        F_AT.append(F_AT[n] + EC * near + HC)
    T_PER, M_PER, F_PER = T_AT[3] - T_AT[2], M_AT[3] - M_AT[2], F_AT[3] - F_AT[2]
    assert (2 * T_PER) % 3 == 0 and M_PER % 2 == 0 and F_PER % 2 == 0

    def t_uses(h):
        return Uses(T_AT[h.n] + 2 * T_PER * h.lap, T_AT[h.n] % 3, 3)

    def m_uses(h):
        return Uses(M_AT[h.n] + 2 * M_PER * h.lap, M_AT[h.n] % 2, 2)

    def f_uses(h):
        return Uses(F_AT[h.n] + 2 * F_PER * h.lap, F_AT[h.n] % 2, 2)

    def after(eng, sem, count):
        if not isinstance(count, int) or count > 0:
            eng.wait_ge(sem, count)

    x_v = x.rearrange("b s e -> (b s) e").rearrange("(n p t) e -> p n t e", p=P, t=NT)
    out_v = out.rearrange("b s e -> (b s) e").rearrange("(n p t) e -> p n t e", p=P, t=NT)

    with ExitStack() as ctx:
        def sb(name, shape, dt=F32):
            return ctx.enter_context(nc.sbuf_tensor(name, shape, dt))

        def sem(name):
            return ctx.enter_context(nc.semaphore(name))

        T = [ctx.enter_context(nc.psum_tensor(f"T{i}", [P, 512], F32)) for i in range(3)]
        M = [ctx.enter_context(nc.psum_tensor(f"M{i}", [P, 512], F32)) for i in range(2)]
        F = [ctx.enter_context(nc.psum_tensor(f"F{i}", [P, 512], F32)) for i in range(2)]
        state = ctx.enter_context(nc.psum_tensor("state", [P, 512], F32))

        ident = sb("ident", [P, P])
        ones = sb("ones", [P, P])
        ones_r = sb("ones_r", [1, P], F32R)
        head_mask = sb("head_mask", [P, HB, HD])
        minus_half = sb("minus_half", [P, 2 * NT])

        wq_hi = sb("wq_hi", [P, EC, E], F32R)
        wq_lo = sb("wq_lo", [P, EC, E], F32R)
        wkv_hi = sb("wkv_hi", [P, EC, 2 * E], F32R)
        wkv_lo = sb("wkv_lo", [P, EC, 2 * E], F32R)
        wo_hi = sb("wo_hi", [P, EC, E], F32R)
        wo_lo = sb("wo_lo", [P, EC, E], F32R)
        w1_t = sb("w1_t", [P, EC, HID], F32R)
        w2_t = sb("w2_t", [P, HC, E], F32R)

        VEC = {"bq": (0, EC), "g1": (EC, EC), "c1": (2 * EC, EC), "b1": (3 * EC, HC),
               "g2": (3 * EC + HC, HC), "c2": (3 * EC + 2 * HC, HC)}
        NV = 3 * EC + 3 * HC
        vec_rows = sb("vec_rows", [NV, P])
        vec = sb("vec", [P, NV])
        bq_plus_1 = sb("bq_plus_1", [P, EC])
        minus_bq = sb("minus_bq", [P, EC])
        gc2 = sb("gc2", [P, HC, 2])
        bk_row = sb("bk_row", [1, E])
        bk_hi = sb("bk_hi", [1, E], F32R)
        bk_lo = sb("bk_lo", [1, E], F32R)
        bv_all = sb("bv_all", [P, E])
        bo_all = sb("bo_all", [P, E])
        b2_all = sb("b2_all", [P, E])
        b1_all = sb("b1_all", [P, HC])
        ce_rows = sb("ce_rows", [2, E])
        pick = sb("pick", [2, 2, P])
        c_all = sb("c_all", [P, E])
        e_all = sb("e_all", [P, E])
        abs_part = sb("abs_part", [P, 2, HC])
        abs_sum = sb("abs_sum", [P, 2])
        mean_abs = sb("mean_abs", [P, 2])
        quant = sb("quant", [P, 2])
        step = sb("step", [P, 2])

        x_in = sb("x_in", [P, 2, NT, E])
        xt_hi = sb("xt_hi", [P, EC, TOK], F32R)
        xt_lo = sb("xt_lo", [P, EC, TOK], F32R)
        exp_q = sb("exp_q", [P, EC, TOK])
        q_t = sb("q_t", [P, 2, EC, TOK])
        exp_k = sb("exp_k", [P, 2, E])
        k_sb = sb("k_sb", [P, NT, E])
        v_sb = sb("v_sb", [P, NT, EC, VW])
        k_sum = sb("k_sum", [P, EC, 1])
        kv_raw = sb("kv_raw", [P, EC, P])
        kv = sb("kv", [P, EC, AW])

        den = sb("den", [P, NT, HEADS])
        inv_den = sb("inv_den", [P, NT, HEADS])
        attn = sb("attn", [P, NT, E])
        at_hi = sb("at_hi", [P, EC, TOK], F32R)
        at_lo = sb("at_lo", [P, EC, TOK], F32R)
        x_bo = sb("x_bo", [P, 2, NT, E])
        y1 = sb("y1", [P, NT, E])
        z = sb("z", [P, NT, E])
        ht_hi = sb("ht_hi", [P, EC, TOK], F32R)
        ht_lo = sb("ht_lo", [P, EC, TOK], F32R)
        g = sb("g", [P, HC, TOK])
        g_hi = sb("g_hi", [P, HC, TOK], F32R)
        g_lo = sb("g_lo", [P, HC, TOK], F32R)
        x1 = sb("x1", [P, NT, E])
        x1_e = sb("x1_e", [P, 2, NT, E])
        f_mid = sb("f_mid", [P, 2, E])
        y2 = sb("y2", [P, NT, E])
        out_sb = sb("out_sb", [P, 2, NT, E])
        st1 = sb("st1", [P, NT, 6])
        mv1 = sb("mv1", [P, NT, 2])
        var1 = sb("var1", [P, 2, NT])
        r1 = sb("r1", [P, 2, NT])
        st2 = sb("st2", [P, NT, 2, 6])
        mv2 = sb("mv2", [P, NT, 2])
        var2 = sb("var2", [P, NT])
        minus_mean2 = sb("minus_mean2", [P, NT])
        r2 = sb("r2", [P, NT])
        r2_step = sb("r2_step", [P, NT])
        st3 = sb("st3", [P, NT, 6])
        mv3 = sb("mv3", [P, NT, 2])
        var3 = sb("var3", [P, NT])
        r3 = sb("r3", [P, NT])

        unused = sb("unused", [P, 4])

        w_raw = [y1, z, attn, y2]
        w1_raw, w2_raw = g[:, 0:4, :], g[:, 4:8, :]
        tern_tmp = x1_e

        x_loaded = [sem("x_loaded_0"), sem("x_loaded_1")]
        w_loaded = [sem(f"w_loaded_{i}") for i in range(4)]
        ffn_loaded = [sem("w1_loaded"), sem("w2_loaded")]
        vec_loaded = sem("vec_loaded")
        rows_loaded = sem("rows_loaded")
        setup_made = sem("setup_made")
        prep = sem("prep")
        w_hi_made = sem("w_hi_made")
        t_filled, t_drained = sem("t_filled"), sem("t_drained")
        m_filled, m_drained = sem("m_filled"), sem("m_drained")
        f_filled = sem("f_filled")
        x_hi_made = sem("x_hi_made")
        relu_q_made = sem("relu_q_made")
        relu_k_made = sem("relu_k_made")
        exp_q_made = sem("exp_q_made")
        q_made = sem("q_made")
        exp_k_made = sem("exp_k_made")
        state_summed = sem("state_summed")
        state_step = sem("state_step")
        kv_made = sem("kv_made")
        attn_step = sem("attn_step")
        a_hi_made = sem("a_hi_made")
        x_bo_made = sem("x_bo_made")
        ln1_step = sem("ln1_step")
        r1_made = sem("r1_made")
        x1_made = sem("x1_made")
        x1_e_made = sem("x1_e_made")
        z_made = sem("z_made")
        h_hi_made = sem("h_hi_made")
        gelu_made = sem("gelu_made")
        g_hi_made = sem("g_hi_made")
        g_lo_made = sem("g_lo_made")
        ln2_step = sem("ln2_step")
        r2_made = sem("r2_made")
        y2_step = sem("y2_step")
        r3_made = sem("r3_made")
        out_made = sem("out_made")
        out_free = [sem("out_free_0"), sem("out_free_1")]

        def vcol(name, k):
            return vec[:, VEC[name][0] + k:VEC[name][0] + k + 1]

        def f32(ap):
            return ap.bitcast(F32)

        block = ctx.enter_context(nc.Block())

        @block.sync
        def _(sp):
            def load_x(h):
                sp.dma_start(x_in[:, h.par], x_v[:, h.at(1)]).then_inc(x_loaded[h.par], 16)

            load_x(Half(0))
            for i, w in enumerate([Wq, Wk, Wv]):
                dst = w_raw[i][:, 0:EC, :]
                sp.dma_start(dst, w.rearrange("(c p) e -> p c e", p=P)).then_inc(w_loaded[i], 16)
            for name, v in (("bq", bq), ("g1", ln1_g), ("c1", ln1_b), ("b1", b1), ("g2", ln2_g), ("c2", ln2_b)):
                at, n = VEC[name]
                sp.dma_start(vec_rows[at:at + n, :], v.rearrange("(c p) -> c p", p=P)).then_inc(vec_loaded, 16)
            sp.dma_start(bk_row[:], bk.rearrange("(a e) -> a e", a=1)).then_inc(rows_loaded, 16)
            for dst, v in ((bv_all, bv), (bo_all, bo), (b2_all, b2)):
                sp.dma_start(dst[:], v.rearrange("(a e) -> a e", a=1).to_broadcast([P, E])).then_inc(rows_loaded, 16)
            sp.dma_start(w1_raw.rearrange("p a (b e) -> p (a b) e", e=E),
                         w1.rearrange("(j p) e -> p j e", p=P)).then_inc(ffn_loaded[0], 16)
            sp.dma_start(w2_raw.rearrange("p (c a) e -> p c (a e)", c=EC),
                         w2.rearrange("(c p) h -> p c h", p=P)).then_inc(ffn_loaded[1], 16)
            sp.dma_start(w_raw[3][:, 0:EC, :], Wo.rearrange("(c p) e -> p c e", p=P)).then_inc(w_loaded[3], 16)
            load_x(Half(1))

            for n in (0, 1):
                sp.wait_ge(t_filled, X_TURNED[n])
                sp.wait_ge(x_bo_made, n + 1)
                load_x(Half(n + 2))

            def half(h):
                if h.n + 4 < NH:
                    sp.wait_ge(t_filled, T_AT[h.n] + EC + 2 * T_PER * h.lap)
                    sp.wait_ge(x_bo_made, h.at(1, 3))
                    load_x(h.ahead(4))
                if h.n >= 1:
                    store(h.ahead(-1))

            def store(h):
                sp.wait_ge(out_made, h.at(NT, NT))
                sp.dma_start(out_v[:, h.at(1)], out_sb[:, h.par]).then_inc(out_free[h.par], 16)

            half(Half(0))
            half(Half(1))
            with sp.Fori(0, LAPS - 1) as lap:
                half(Half(2, lap))
                half(Half(3, lap))
            for n in range(2 * LAPS, NH):
                half(Half(n))
            store(Half(NH - 1))
            for par in (0, 1):
                sp.wait_ge(out_free[par], 16 * (NH // 2 + 1))

        @block.gpsimd
        def _(pool):
            pool.memset(ident[:], 0.0).then_inc(setup_made, 1)
            pool.memset(head_mask[:], 1.0).then_inc(setup_made, 1)
            pool.wait_ge(setup_made, 2)
            pool.affine_select(out=ident[:], in_=ident[:], compare_op=ALU.not_equal, fill=1.0, base=0,
                               pattern=[[-1, P]], channel_multiplier=1).then_inc(setup_made, 1)
            pool.affine_select(out=head_mask[:], in_=head_mask[:], compare_op=ALU.is_ge, fill=0.0, base=0,
                               pattern=[[-HD, HB], [0, HD]], channel_multiplier=1).then_inc(setup_made, 1)
            pool.wait_ge(setup_made, 4)
            pool.affine_select(out=head_mask[:], in_=head_mask[:], compare_op=ALU.is_ge, fill=0.0, base=HD - 1,
                               pattern=[[HD, HB], [0, HD]], channel_multiplier=-1).then_inc(setup_made, 1)
            pool.memset(ones[:], 1.0).then_inc(setup_made, 1)
            pool.memset(f32(ones_r[:]), 1.0).then_inc(setup_made, 1)
            pool.memset(minus_half[:], -0.5).then_inc(setup_made, 1)
            pool.memset(v_sb[:], 1.0).then_inc(setup_made, 1)
            pool.wait_ge(setup_made, 9)

            def rows_plus_bo(h):
                pool.wait_ge(x_loaded[h.par], 16 * (h.n // 2 + 1) + 16 * h.lap)
                pool.tensor_tensor(x_bo[:, h.par], x_in[:, h.par], bo_all[:, None, :].to_broadcast([P, NT, E]),
                                   ALU.add).then_inc(x_bo_made, 1)

            pool.wait_ge(rows_loaded, 64)
            rows_plus_bo(Half(0))
            rows_plus_bo(Half(1))

            def power2(h):
                pool.wait_ge(ln2_step, h.at(NT + 2, NT + 2))
                pool.tensor_tensor(r2[:], var2[:], minus_half[:, 0:NT], ALU.pow).then_inc(r2_made, 1)
                pool.wait_ge(r2_made, h.at(2, 1))
                pool.tensor_tensor(r2_step[:], r2[:], step[:, 1:2].to_broadcast([P, NT]), ALU.mult).then_inc(r2_made, 1)

            def power3(h):
                pool.wait_ge(y2_step, h.at(3 * NT + 1, 3 * NT + 1))
                pool.tensor_tensor(r3[:], var3[:], minus_half[:, 0:NT], ALU.pow).then_inc(r3_made, 1)

            def half(h):
                if h.n >= 1:
                    power2(h.ahead(-1))
                pool.wait_ge(ln1_step, h.at(2 * NT + 2, 2 * NT + 2))
                pool.tensor_tensor(r1[:].rearrange("p a t -> p (a t)"), var1[:].rearrange("p a t -> p (a t)"),
                                   minus_half[:], ALU.pow).then_inc(r1_made, 1)
                pool.wait_ge(r1_made, h.at(1, 1))
                if h.n < NH - 2:
                    rows_plus_bo(h.ahead(2))
                for t in range(NT):
                    ins = pool.tensor_scalar(x1[:, t], y1[:, t], mv1[:, t, 0:1], r1[:, 0, t:t + 1],
                                             ALU.subtract, ALU.mult)
                    ins.then_inc(x1_made, 1)
                pool.wait_ge(x1_made, h.at(NT, NT))
                pool.tensor_tensor(x1_e[:, h.par], x1[:], e_all[:, None, :].to_broadcast([P, NT, E]),
                                   ALU.add).then_inc(x1_e_made, 1)
                if h.n >= 1:
                    power3(h.ahead(-1))

            pool.wait_ge(prep, PREP_END)
            half(Half(0))
            half(Half(1))
            with pool.Fori(0, LAPS) as lap:
                half(Half(2, lap))
                half(Half(3, lap))
            for n in TAIL:
                half(Half(n))
            power2(Half(NH - 1))
            power3(Half(NH - 1))

        @block.tensor
        def _(pe):
            def turn(tu, tiles):
                u, bank = tu.take()
                after(pe, t_drained, u - 2)
                for at, src in tiles:
                    mm = pe.transpose(T[bank][:, at * P:at * P + P], src, ident[:])
                mm.then_inc(t_filled, 1)

            def turn_x(h, tu):
                pe.wait_ge(x_loaded[h.par], 16 * (h.n // 2 + 1) + 16 * h.lap)
                for c in range(EC):
                    turn(tu, [(t, x_in[:, h.par, t, c * P:c * P + P]) for t in range(NT)])

            def project_q(h, fu, x_turned):
                pe.wait_ge(t_drained, x_turned)
                for c in range(EC):
                    _, bank = fu.take()
                    if h.n >= 3:
                        pe.wait_ge(gelu_made, h.ahead(-3).at(HC, HC - EC + c + 1))
                    elif h.n >= 1:
                        pe.wait_ge(q_made, (h.n - 1) * EC + c + 1)
                    k = 0
                    for ec in range(EC):
                        for w, xt in ((wq_hi, xt_hi), (wq_hi, xt_lo), (wq_lo, xt_hi)):
                            mm = pe.matmul(F[bank][:], w[:, ec, c * P:c * P + P], xt[:, ec],
                                           start=(k == 0), stop=(k == 3 * EC - 1))
                            k += 1
                    mm.then_inc(f_filled, 1)

            def project_kv(t, mu):
                u, bank = mu.take()
                after(pe, m_drained, u - 1)
                k = 0
                for ec in range(EC):
                    for xt, w in ((xt_hi, wkv_hi), (xt_lo, wkv_hi), (xt_hi, wkv_lo)):
                        pe.matmul(M[bank][:], xt[:, ec, t * P:t * P + P], w[:, ec], start=(k == 0), stop=False)
                        k += 1
                pe.matmul(M[bank][:, 0:E], ones_r[:], bk_hi[:], start=False, stop=False)
                pe.matmul(M[bank][:, 0:E], ones_r[:], bk_lo[:], start=False, stop=True).then_inc(m_filled, 1)

            def sum_state(h, kv_drained):
                if h.par == 0 and h.n >= 2:
                    pe.wait_ge(kv_made, (h.n // 2) * 2 * EC + 2 * EC * h.lap)
                pe.wait_ge(m_drained, kv_drained)
                for t in range(NT):
                    for c in range(EC):
                        first = h.par == 0 and t == 0
                        last = h.par == 1 and t == NT - 1
                        mm = pe.matmul(state[:, c * AW:c * AW + P + 1], k_sb[:, t, c * P:c * P + P],
                                       v_sb[:, t, c, 0:P + 1], start=first and c == 0, stop=last,
                                       skip_group_check=True)
                if h.par == 1:
                    mm.then_inc(state_summed, 1)

            def attend(h, tu):
                pe.wait_ge(kv_made, (h.n // 2 + 1) * 2 * EC + 2 * EC * h.lap)
                pe.wait_ge(q_made, h.at(EC, EC))
                for t in range(NT):
                    u, bank = tu.take()
                    pe.wait_ge(t_drained, u - 2)
                    for c in range(EC):
                        mm = pe.matmul(T[bank][:, c * AW:c * AW + AW], q_t[:, h.par, c, t * P:t * P + P],
                                       kv[:, c], start=True, stop=True)
                    mm.then_inc(t_filled, 1)

            def project_o(t, mu):
                u, bank = mu.take()
                pe.wait_ge(m_drained, u - 1)
                k = 0
                for ec in range(EC):
                    for a, w in ((at_hi, wo_hi), (at_lo, wo_hi), (at_hi, wo_lo)):
                        mm = pe.matmul(M[bank][:, 0:E], a[:, ec, t * P:t * P + P], w[:, ec],
                                       start=(k == 0), stop=(k == 3 * EC - 1))
                        k += 1
                mm.then_inc(m_filled, 1)

            def turn_gelu(h, part, t, tu):
                pe.wait_ge(gelu_made, h.at(HC, part * 4 + 4))
                turn(tu, [(i, g[:, part * 4 + i, t * P:t * P + P]) for i in range(4)])

            def feed_1(h, j, fu):
                _, bank = fu.take()
                if j >= EC:
                    pe.wait_ge(gelu_made, h.at(HC, j - 1))
                elif h.n < NH - 2:
                    pe.wait_ge(q_made, h.ahead(2).at(EC, j + 1))
                else:
                    pe.wait_ge(gelu_made, h.ahead(-1).at(HC, HC - EC + j + 1))
                k = 0
                for ec in range(EC):
                    for part in (ht_hi, ht_lo):
                        mm = pe.matmul(F[bank][:], w1_t[:, ec, j * P:j * P + P], part[:, ec],
                                       start=(k == 0), stop=(k == 2 * EC - 1))
                        k += 1
                mm.then_inc(f_filled, 1)

            def feed_2(h, mu):
                pe.wait_ge(g_lo_made, h.at(HC, HC))
                for t in range(NT):
                    u, bank = mu.take()
                    pe.wait_ge(m_drained, u - 1)
                    for j in range(HC):
                        for part in (g_hi, g_lo):
                            mm = pe.matmul(M[bank][:, 0:E], part[:, j, t * P:t * P + P], w2_t[:, j],
                                           start=(j == 0 and part is g_hi), stop=(j == HC - 1 and part is g_lo))
                    mm.then_inc(m_filled, 1)

            pe.wait_ge(setup_made, 9)
            tu, mu, fu = Uses(0, 0, 3), Uses(0, 0, 2), Uses(0, 0, 2)

            def turn_square(i):
                pe.wait_ge(w_loaded[i], 16)
                turn(tu, [(ec * EC + oc, w_raw[i][:, oc, ec * P:ec * P + P]) for ec in range(EC) for oc in range(EC)])

            for i in range(3):
                turn_square(i)
            pe.wait_ge(vec_loaded, 6 * 16)
            u, bank = tu.take()
            pe.wait_ge(t_drained, u - 2)
            pe.transpose(T[bank][:, 0:NV], vec_rows[:], ident[0:NV, 0:NV]).then_inc(t_filled, 1)
            turn_x(Half(0), tu)
            pe.wait_ge(prep, PREP_BK)
            project_q(Half(0), fu, tu.first + tu.k)
            for t in range(NT):
                project_kv(t, mu)
            sum_state(Half(0), NT)
            pe.wait_ge(prep, PREP_ABS)
            u, bank = tu.take()
            pe.wait_ge(t_drained, u - 2)
            pe.matmul(T[bank][:, 0:2], ones[:], abs_sum[:], start=True, stop=True).then_inc(t_filled, 1)
            turn_square(3)
            pe.wait_ge(prep, PREP_TERN1)
            w1_q = w1_raw.rearrange("p a (b e) -> p (a b) e", e=E)
            for ec in range(EC):
                for q in range(2):
                    turn(tu, [(i, w1_q[:, 4 * q + i, ec * P:ec * P + P]) for i in range(4)])
            pe.wait_ge(prep, PREP_TERN2)
            w2_q = w2_raw.rearrange("p (c a) e -> p c (a e)", c=EC)
            for q in range(4):
                turn(tu, [(i * EC + dc, w2_q[:, dc, (2 * q + i) * P:(2 * q + i) * P + P])
                          for i in range(2) for dc in range(EC)])
            turn_x(Half(1), tu)
            project_q(Half(1), fu, tu.first + tu.k)
            for t in range(NT):
                project_kv(t, mu)
            sum_state(Half(1), 2 * NT)
            u, bank = tu.take()
            pe.wait_ge(t_drained, u - 2)
            for j in range(HC):
                for ec in range(EC):
                    mm = pe.matmul(T[bank][:, j:j + 1], f32(w1_t[:, ec, j * P:j * P + P]), vcol("c1", ec),
                                   start=(ec == 0), stop=(ec == EC - 1))
            mm.then_inc(t_filled, 1)
            u, bank = tu.take()
            pe.wait_ge(t_drained, u - 2)
            for j in range(HC):
                mm = pe.matmul(T[bank][0:2, 0:E], gc2[:, j], f32(w2_t[:, j]), start=(j == 0), stop=(j == HC - 1))
            mm.then_inc(t_filled, 1)
            pe.wait_ge(t_drained, u + 1)
            u, bank = tu.take()
            for i in range(2):
                mm = pe.matmul(T[bank][:, i * E:i * E + E], pick[:, i], ce_rows[:], start=True, stop=True)
            mm.then_inc(t_filled, 1)
            assert tu.k == T_PRO and mu.k == M_PRO and fu.k == F_PRO

            def half(h):
                tu, mu, fu = t_uses(h), m_uses(h), f_uses(h)
                near, late = h.n < NH - 2, h.n >= 1
                if near:
                    turn_x(h.ahead(2), tu)
                    x_turned = tu.first + tu.k
                attend(h, tu)
                if near:
                    project_q(h.ahead(2), fu, x_turned)
                attn_drained = tu.first + tu.k
                pe.wait_ge(t_drained, attn_drained)
                for c in range(EC):
                    turn(tu, [(t, attn[:, t, c * P:c * P + P]) for t in range(NT)])
                a_turned = tu.first + tu.k
                for t in range(NT):
                    if late:
                        turn_gelu(h.ahead(-1), 1, t, tu)
                    if near:
                        project_kv(t, mu)
                kv_drained = mu.first + mu.k
                pe.wait_ge(t_drained, a_turned)
                for t in range(NT):
                    project_o(t, mu)
                if near:
                    sum_state(h.ahead(2), kv_drained)
                if late:
                    feed_2(h.ahead(-1), mu)
                pe.wait_ge(z_made, h.at(NT, NT))
                for c in range(EC):
                    turn(tu, [(t, z[:, t, c * P:c * P + P]) for t in range(NT)])
                pe.wait_ge(t_drained, tu.first + tu.k)
                for j in range(HC):
                    feed_1(h, j, fu)
                    if j >= 4:
                        turn_gelu(h, 0, j - 4, tu)

            half(Half(0))
            half(Half(1))
            with pe.Fori(0, LAPS) as lap:
                half(Half(2, lap))
                half(Half(3, lap))
            for n in TAIL:
                half(Half(n))
            tu, mu = t_uses(Half(NH)), m_uses(Half(NH))
            for t in range(NT):
                turn_gelu(Half(NH - 1), 1, t, tu)
            feed_2(Half(NH - 1), mu)

        @block.scalar
        def _(act):
            def hi_parts(sem_made, dst, tu, scale=None):
                for c in range(EC):
                    u, bank = tu.take()
                    act.wait_ge(t_filled, u + 1)
                    act.activation(dst[:, c], T[bank][:], ACT.Identity,
                                   scale=1.0 if scale is None else vcol(scale, c)).then_inc(sem_made, 1)

            def exps_q(h, fu):
                for c in range(EC):
                    u, bank = fu.take()
                    act.wait_ge(f_filled, u + 1)
                    after(act, q_made, h.ahead(-1).at(EC, c + 1))
                    act.activation(exp_q[:, c], F[bank][:], ACT.Relu, scale=-1.0,
                                   bias=minus_bq[:, c:c + 1]).then_inc(relu_q_made, 1)
                    act.wait_ge(relu_q_made, h.at(EC, c + 1))
                    act.activation(exp_q[:, c], exp_q[:, c], ACT.Exp, scale=-1.0).then_inc(exp_q_made, 1)

            def keys_values(h, t, mu):
                u, bank = mu.take()
                act.wait_ge(m_filled, u + 1)
                act.activation(v_sb[:, t, :, 0:P], M[bank][:, E:2 * E].rearrange("p (c m) -> p c m", c=EC),
                               ACT.Identity)
                after(act, m_drained, u - 1)
                act.activation(exp_k[:, t % 2], M[bank][:, 0:E], ACT.Relu, scale=-1.0,
                               bias=ones[:, 0:1]).then_inc(relu_k_made, 1)
                act.wait_ge(relu_k_made, h.at(NT, t + 1))
                act.activation(exp_k[:, t % 2], exp_k[:, t % 2], ACT.Exp, scale=-1.0).then_inc(exp_k_made, 1)

            tu, mu, fu = Uses(0, 0, 3), Uses(0, 0, 2), Uses(0, 0, 2)

            def weight_hi(dst):
                u, bank = tu.take()
                act.wait_ge(t_filled, u + 1)
                act.activation(dst, T[bank][:].rearrange("p (c e) -> p c e", c=EC),
                               ACT.Identity).then_inc(w_hi_made, 1)

            act.wait_ge(setup_made, 9)
            weight_hi(wq_hi[:])
            weight_hi(wkv_hi[:, :, 0:E])
            weight_hi(wkv_hi[:, :, E:2 * E])
            tu.take()
            hi_parts(x_hi_made, xt_hi, tu)
            act.wait_ge(prep, PREP_VEC)
            exps_q(Half(0), fu)
            for t in range(NT):
                keys_values(Half(0), t, mu)
            tu.take()
            weight_hi(wo_hi[:])
            for _ in range(8):
                tu.take()
            hi_parts(x_hi_made, xt_hi, tu)
            exps_q(Half(1), fu)
            for t in range(NT):
                keys_values(Half(1), t, mu)
            act.wait_ge(prep, PREP_END)

            def half(h):
                tu, mu, fu = t_uses(h), m_uses(h), f_uses(h)
                near, late = h.n < NH - 2, h.n >= 1
                if near:
                    hi_parts(x_hi_made, xt_hi, tu)
                for t in range(NT):
                    tu.take()
                if near:
                    exps_q(h.ahead(2), fu)
                hi_parts(a_hi_made, at_hi, tu)
                for t in range(NT):
                    if late:
                        tu.take()
                    if near:
                        keys_values(h.ahead(2), t, mu)
                hi_parts(h_hi_made, ht_hi, tu, scale="g1")
                for j in range(HC):
                    u, bank = fu.take()
                    act.wait_ge(f_filled, u + 1)
                    if late and j % 4 == 0:
                        act.wait_ge(g_lo_made, h.ahead(-1).at(HC, j + 4))
                    act.activation(g[:, j], F[bank][:], ACT.Gelu, scale=step[:, 0:1],
                                   bias=b1_all[:, j:j + 1]).then_inc(gelu_made, 1)
                    act.wait_ge(gelu_made, h.at(HC, j + 1))
                    act.activation(g_hi[:, j], g[:, j], ACT.Identity, scale=vcol("g2", j)).then_inc(g_hi_made, 1)

            half(Half(0))
            half(Half(1))
            with act.Fori(0, LAPS) as lap:
                half(Half(2, lap))
                half(Half(3, lap))
            for n in TAIL:
                half(Half(n))

        @block.vector
        def _(dve):
            def lo_parts(sem_made, made, hi, lo, tu, scale=None):
                for c in range(EC):
                    u, bank = tu.take()
                    dve.wait_ge(sem_made, made + c + 1)
                    if scale is None:
                        ins = dve.tensor_tensor(lo[:, c], T[bank][:], f32(hi[:, c]), ALU.subtract)
                    else:
                        ins = dve.scalar_tensor_tensor(lo[:, c], T[bank][:], vcol(scale, c), f32(hi[:, c]),
                                                       ALU.mult, ALU.subtract)
                    ins.then_inc(t_drained, 1)

            def make_q(h, fu):
                for c in range(EC):
                    _, bank = fu.take()
                    dve.wait_ge(exp_q_made, h.at(EC, c + 1))
                    dve.scalar_tensor_tensor(q_t[:, h.par, c], F[bank][:], bq_plus_1[:, c:c + 1], exp_q[:, c],
                                             ALU.add, ALU.max).then_inc(q_made, 1)

            def make_k(h, t, mu):
                _, bank = mu.take()
                dve.wait_ge(exp_k_made, h.at(NT, t + 1))
                dve.tensor_tensor(k_sb[:, t], exp_k[:, t % 2], M[bank][:, 0:E], ALU.max).then_inc(m_drained, 1)

            def carry_wait():
                dve.memset(unused[:, 3:4], 0.0)

            def make_kv(h):
                done = (h.n // 2) + h.lap
                dve.wait_ge(state_summed, done + 1)
                sums = state[:, 0:EC * AW].rearrange("p (c w) -> p c w", c=EC)
                dve.tensor_copy(k_sum[:], sums[:, :, P:P + 1]).then_inc(state_step, 1)
                dve.wait_ge(state_step, 3 * done + 1)
                for c in range(EC):
                    dve.scalar_tensor_tensor(kv_raw[:, c], bv_all[:, c * P:c * P + P], k_sum[:, c],
                                             state[:, c * AW:c * AW + P], ALU.mult, ALU.add).then_inc(state_step, 1)
                dve.wait_ge(state_step, 3 * done + 3)
                for c in range(EC):
                    dve.tensor_tensor(kv[:, c, 0:P], kv_raw[:, c], head_mask[:].rearrange("p h m -> p (h m)"),
                                      ALU.mult).then_inc(kv_made, 1)
                    dve.tensor_scalar(kv[:, c, P:AW], head_mask[:, :, 0], k_sum[:, c], None,
                                      ALU.mult).then_inc(kv_made, 1)

            def make_attn(h, tu):
                for t in range(NT):
                    u, bank = tu.take()
                    sums = T[bank][:, 0:EC * AW].rearrange("p (c w) -> p c w", c=EC)
                    dve.wait_ge(t_filled, u + 1)
                    dve.tensor_scalar(den[:, t].rearrange("p (c h) -> p c h", c=EC), sums[:, :, P:AW], ATTN_EPS, None,
                                      ALU.add).then_inc(attn_step, 1)
                    dve.wait_ge(attn_step, h.at(2 * NT, 2 * t + 1))
                    dve.reciprocal(inv_den[:, t], den[:, t]).then_inc(attn_step, 1)
                    dve.wait_ge(attn_step, h.at(2 * NT, 2 * t + 2))
                    dve.tensor_tensor(attn[:, t].rearrange("p (c h m) -> p c h m", c=EC, h=HB),
                                      sums[:, :, 0:P].rearrange("p c (h m) -> p c h m", h=HB),
                                      inv_den[:, t].rearrange("p (c h) -> p c h", c=EC)[:, :, :, None]
                                      .to_broadcast([P, EC, HB, HD]), ALU.mult).then_inc(t_drained, 1)

            def gelu_stats(part, t, tu):
                u, bank = tu.take()
                dve.wait_ge(t_filled, u + 1)
                dve.bn_stats(st2[:, t, part], T[bank][:]).then_inc(t_drained, 1)

            def gelu_moments(h, stats_drained):
                dve.wait_ge(t_drained, stats_drained)
                after(dve, r2_made, h.at(2, 0))
                carry_wait()
                for t in range(NT):
                    dve.bn_aggr(mv2[:, t], st2[:, t].rearrange("p a s -> p (a s)")).then_inc(ln2_step, 1)
                dve.wait_ge(ln2_step, h.at(NT + 2, NT))
                dve.tensor_scalar(var2[:], mv2[:, :, 1], LN_EPS, None, ALU.add).then_inc(ln2_step, 1)
                dve.tensor_scalar(minus_mean2[:], mv2[:, :, 0], -1.0, None, ALU.mult).then_inc(ln2_step, 1)

            def make_y1(h, mu):
                dve.wait_ge(x_bo_made, h.at(1, 1))
                after(dve, x1_made, h.at(NT, 0))
                at = 0
                for t in range(NT):
                    u, bank = mu.take()
                    dve.wait_ge(m_filled, u + 1)
                    dve.tensor_tensor(y1[:, t], M[bank][:, 0:E], x_bo[:, h.par, t], ALU.add).then_inc(m_drained, 1)
                    dve.wait_ge(m_drained, u + 1)
                    dve.bn_stats(st1[:, t], y1[:, t]).then_inc(ln1_step, 1)
                dve.wait_ge(ln1_step, h.at(2 * NT + 2, NT))
                carry_wait()
                for t in range(NT):
                    dve.bn_aggr(mv1[:, t], st1[:, t]).then_inc(ln1_step, 1)
                dve.wait_ge(ln1_step, h.at(2 * NT + 2, 2 * NT))
                dve.tensor_scalar(var1[:, 0], mv1[:, :, 1], LN_EPS, None, ALU.add).then_inc(ln1_step, 1)
                dve.tensor_scalar(var1[:, 1], mv1[:, :, 1], 1.0 + LN_EPS, LN_EPS * LN_EPS, ALU.mult,
                                  ALU.add).then_inc(ln1_step, 1)

            def make_z(h):
                dve.wait_ge(r1_made, h.at(1, 1))
                for t in range(NT):
                    dve.tensor_scalar(z[:, t], y1[:, t], mv1[:, t, 0:1], r1[:, 1, t:t + 1], ALU.subtract,
                                      ALU.mult).then_inc(z_made, 1)

            def make_y2(h, t, mu):
                Y = 3 * NT + 1
                u, bank = mu.take()
                if t == 0:
                    dve.wait_ge(r2_made, h.at(2, 2))
                    dve.wait_ge(x1_e_made, h.at(1, 1))
                dve.wait_ge(m_filled, u + 1)
                dve.scalar_tensor_tensor(f_mid[:, t % 2], c_all[:], minus_mean2[:, t:t + 1], M[bank][:, 0:E],
                                         ALU.mult, ALU.add).then_inc(m_drained, 1)
                dve.wait_ge(m_drained, u + 1)
                dve.scalar_tensor_tensor(y2[:, t], f_mid[:, t % 2], r2_step[:, t:t + 1], x1_e[:, h.par, t],
                                         ALU.mult, ALU.add).then_inc(y2_step, 1)
                dve.wait_ge(y2_step, h.at(Y, 2 * t + 1))
                dve.bn_stats(st3[:, t], y2[:, t]).then_inc(y2_step, 1)
                if t == NT - 1:
                    dve.wait_ge(y2_step, h.at(Y, 2 * NT))
                    carry_wait()
                    for i in range(NT):
                        dve.bn_aggr(mv3[:, i], st3[:, i]).then_inc(y2_step, 1)
                    dve.wait_ge(y2_step, h.at(Y, 3 * NT))
                    dve.tensor_scalar(var3[:], mv3[:, :, 1], LN_EPS, None, ALU.add).then_inc(y2_step, 1)

            def make_out(h):
                dve.wait_ge(r3_made, h.at(1, 1))
                dve.wait_ge(out_free[h.par], 16 * (h.n // 2 + 1) + 16 * h.lap)
                for t in range(NT):
                    dve.tensor_scalar(out_sb[:, h.par, t], y2[:, t], mv3[:, t, 0:1], r3[:, t:t + 1], ALU.subtract,
                                      ALU.mult).then_inc(out_made, 1)

            def make_g_lo(h, j):
                dve.wait_ge(g_hi_made, h.at(HC, j + 1))
                dve.scalar_tensor_tensor(g_lo[:, j], g[:, j], vcol("g2", j), f32(g_hi[:, j]), ALU.mult,
                                         ALU.subtract).then_inc(g_lo_made, 1)

            steps = [0]

            def done(ins):
                steps[0] += 1
                ins.then_inc(prep, 1)

            def settled():
                dve.wait_ge(prep, steps[0])

            tu, mu, fu = Uses(0, 0, 3), Uses(0, 0, 2), Uses(0, 0, 2)

            def weight_lo(n, hi, lo):
                u, bank = tu.take()
                dve.wait_ge(w_hi_made, n)
                dve.tensor_tensor(lo, T[bank][:].rearrange("p (c e) -> p c e", c=EC), f32(hi),
                                  ALU.subtract).then_inc(t_drained, 1)

            dve.wait_ge(setup_made, 9)
            weight_lo(1, wq_hi[:], wq_lo[:])
            weight_lo(2, wkv_hi[:, :, 0:E], wkv_lo[:, :, 0:E])
            weight_lo(3, wkv_hi[:, :, E:2 * E], wkv_lo[:, :, E:2 * E])
            u, bank = tu.take()
            dve.wait_ge(t_filled, u + 1)
            dve.tensor_copy(vec[:], T[bank][:, 0:NV]).then_inc(t_drained, 1)
            dve.wait_ge(t_drained, u + 1)
            done(dve.tensor_scalar(bq_plus_1[:], vec[:, 0:EC], 1.0, None, ALU.add))
            done(dve.tensor_scalar(minus_bq[:], vec[:, 0:EC], -1.0, None, ALU.mult))
            done(dve.tensor_copy(gc2[:, :, 0], vec[:, VEC["g2"][0]:VEC["g2"][0] + HC]))
            done(dve.tensor_copy(gc2[:, :, 1], vec[:, VEC["c2"][0]:VEC["c2"][0] + HC]))
            dve.wait_ge(rows_loaded, 64)
            done(dve.tensor_scalar(bk_row[:], bk_row[:], 1.0, None, ALU.add))
            assert steps[0] == PREP_VEC
            settled()
            done(dve.tensor_copy(bk_hi[:], bk_row[:]))
            settled()
            done(dve.tensor_tensor(bk_lo[:], bk_row[:], f32(bk_hi[:]), ALU.subtract))
            assert steps[0] == PREP_BK
            lo_parts(x_hi_made, 0, xt_hi, xt_lo, tu)
            make_q(Half(0), fu)
            for t in range(NT):
                make_k(Half(0), t, mu)

            for i, w in enumerate((w1_raw, w2_raw)):
                dve.wait_ge(ffn_loaded[i], 16)
                done(dve.tensor_reduce(abs_part[:, i], w.rearrange("p a (b e) -> p (a b) e", e=E), AX.X, ALU.add,
                                       apply_absolute_value=True))
            settled()
            done(dve.tensor_reduce(abs_sum[:], abs_part[:], AX.X, ALU.add))
            assert steps[0] == PREP_ABS
            u, bank = tu.take()
            dve.wait_ge(t_filled, u + 1)
            dve.tensor_scalar(mean_abs[:], T[bank][:, 0:2], 1.0 / (E * HID), SCALE_FLOOR, ALU.mult,
                              ALU.max).then_inc(t_drained, 1)
            weight_lo(4, wo_hi[:], wo_lo[:])
            dve.wait_ge(t_drained, u + 1)
            done(dve.reciprocal(quant[:], mean_abs[:]))
            settled()
            done(dve.reciprocal(step[:], quant[:]))
            for i, w in enumerate((w1_raw, w2_raw)):
                tmp = tern_tmp[:].rearrange("p a t e -> p (a t e)").rearrange("p (a b) -> p a b", a=4)
                done(dve.tensor_scalar(tmp, w, quant[:, i:i + 1], -0.5, ALU.mult, ALU.is_lt))
                settled()
                done(dve.tensor_scalar(w, w, quant[:, i:i + 1], 0.5, ALU.mult, ALU.is_gt))
                settled()
                done(dve.tensor_tensor(w, w, tmp, ALU.subtract))
                settled()
                assert steps[0] == (PREP_TERN1, PREP_TERN2)[i]
            for ec in range(EC):
                for q in range(2):
                    u, bank = tu.take()
                    dve.wait_ge(t_filled, u + 1)
                    dve.tensor_copy(w1_t[:, ec, q * 512:q * 512 + 512], T[bank][:]).then_inc(t_drained, 1)
            for q in range(4):
                u, bank = tu.take()
                dve.wait_ge(t_filled, u + 1)
                dve.tensor_copy(w2_t[:, 2 * q:2 * q + 2], T[bank][:].rearrange("p (i e) -> p i e", i=2)
                                ).then_inc(t_drained, 1)
            lo_parts(x_hi_made, EC, xt_hi, xt_lo, tu)
            make_q(Half(1), fu)
            for t in range(NT):
                make_k(Half(1), t, mu)
            make_kv(Half(1))
            u, bank = tu.take()
            dve.wait_ge(t_filled, u + 1)
            dve.scalar_tensor_tensor(b1_all[:], T[bank][:, 0:HC], step[:, 0:1], vec[:, VEC["b1"][0]:VEC["b1"][0] + HC],
                                     ALU.mult, ALU.add).then_inc(t_drained, 1)
            for i in range(2):
                done(dve.tensor_scalar(pick[:, i], ones[0:2, :], ident[0:2, i:i + 1], None, ALU.mult))
            settled()
            u, bank = tu.take()
            dve.wait_ge(t_filled, u + 1)
            dve.tensor_copy(ce_rows[:], T[bank][0:2, 0:E]).then_inc(t_drained, 1)
            u, bank = tu.take()
            dve.wait_ge(t_filled, u + 1)
            done(dve.tensor_copy(c_all[:], T[bank][:, 0:E]))
            dve.scalar_tensor_tensor(e_all[:], T[bank][:, E:2 * E], step[:, 1:2], b2_all[:], ALU.mult,
                                     ALU.add).then_inc(t_drained, 1)
            dve.wait_ge(t_drained, u + 1)
            for par in (0, 1):
                dve.memset(unused[:, par:par + 1], 0.0).then_inc(out_free[par], 16)
            done(dve.memset(unused[:, 2:3], 0.0))
            assert steps[0] == PREP_END and tu.k == T_PRO

            def half(h):
                tu, mu, fu = t_uses(h), m_uses(h), f_uses(h)
                near, late = h.n < NH - 2, h.n >= 1
                if near:
                    lo_parts(x_hi_made, h.ahead(2).at(EC), xt_hi, xt_lo, tu)
                make_attn(h, tu)
                if near:
                    make_q(h.ahead(2), fu)
                lo_parts(a_hi_made, h.at(EC), at_hi, at_lo, tu)
                for t in range(NT):
                    if late:
                        gelu_stats(1, t, tu)
                    if near:
                        make_k(h.ahead(2), t, mu)
                if late:
                    gelu_moments(h.ahead(-1), tu.first + tu.k)
                make_y1(h, mu)
                if near and h.par == 1:
                    make_kv(h.ahead(2))
                if late:
                    make_y2(h.ahead(-1), 0, mu)
                make_z(h)
                if late:
                    for t in range(1, NT):
                        make_y2(h.ahead(-1), t, mu)
                lo_parts(h_hi_made, h.at(EC), ht_hi, ht_lo, tu, scale="g1")
                if late:
                    make_out(h.ahead(-1))
                for j in range(HC):
                    make_g_lo(h, j)
                    if j >= 4:
                        gelu_stats(0, j - 4, tu)

            half(Half(0))
            half(Half(1))
            with dve.Fori(0, LAPS) as lap:
                half(Half(2, lap))
                half(Half(3, lap))
            for n in TAIL:
                half(Half(n))
            last = Half(NH - 1)
            tu, mu = t_uses(Half(NH)), m_uses(Half(NH))
            for t in range(NT):
                gelu_stats(1, t, tu)
            gelu_moments(last, tu.first + tu.k)
            for t in range(NT):
                make_y2(last, t, mu)
            make_out(last)


PREP_VEC = 5
PREP_BK = 7
PREP_ABS = 10
PREP_TERN1 = 15
PREP_TERN2 = 18
PREP_END = 22
X_TURNED = (6, 18)
LAPS = 6
TAIL = (14, 15)

_INS = ['L0_attn_hidden_states', 'L0_attn_Wq', 'L0_attn_bq', 'L0_attn_Wk', 'L0_attn_bk', 'L0_attn_Wv', 'L0_attn_bv',
        'L0_attn_Wo', 'L0_attn_bo', 'L0_ffn_ln1_g', 'L0_ffn_ln1_b', 'L0_ffn_w1', 'L0_ffn_b1', 'L0_ffn_ln2_g',
        'L0_ffn_ln2_b', 'L0_ffn_w2', 'L0_ffn_b2']


def kernel(**inputs):
    import numpy as _np
    import concourse.bacc as _bacc
    from concourse import mybir as _mybir
    from concourse.bass_utils import run_bass_kernel_spmd as _run

    nc = _bacc.Bacc("TRN2", target_bir_lowering=False, num_devices=1)
    arrays, args = {}, []
    for name in _INS:
        a = _np.ascontiguousarray(inputs[name])
        arrays[f"in_{name}"] = a
        args.append(nc.dram_tensor(f"in_{name}", a.shape, _mybir.dt.from_np(a.dtype), kind="ExternalInput").ap())
    shape = inputs['L0_attn_hidden_states'].shape
    args.append(nc.dram_tensor("out_0", shape, _mybir.dt.float32, kind="ExternalOutput").ap())
    block_kernel(nc, *args)
    r = _run(nc, [arrays], core_ids=[0])
    return r.results[0]["out_0"]
```

```python
from contextlib import ExitStack

import concourse.bass as bass
from concourse import mybir

F32 = mybir.dt.float32
F32R = mybir.dt.float32r
ALU = mybir.AluOpType
ACT = mybir.ActivationFunctionType
AX = mybir.AxisListType

P = 128
ATTN_EPS = 1e-6
LN_EPS = 1e-5
SCALE_FLOOR = 1e-5


class Uses:

    def __init__(self, first, bank, banks):
        self.first, self.bank, self.banks, self.k = first, bank, banks, 0

    def take(self):
        k = self.k
        self.k += 1
        return self.first + k, (self.bank + k) % self.banks


class Half:

    def __init__(self, n, lap=0):
        self.n, self.lap, self.par = n, lap, n % 2

    def at(self, per_half, k=0):
        return per_half * self.n + k + 2 * per_half * self.lap

    def ahead(self, d):
        return Half(self.n + d, self.lap)


def block_kernel(nc, x, Wq, bq, Wk, bk, Wv, bv, Wo, bo, ln1_g, ln1_b, w1, b1, ln2_g, ln2_b, w2, b2, out):
    B, S, E = x.shape
    HID = w1.shape[0]
    HEADS = 16
    HD = E // HEADS
    TOK = 512
    NH = B * S // TOK
    NT = TOK // P
    EC = E // P
    HC = HID // P
    HB = P // HD
    AW = P + HB
    VW = P + 4
    assert S == 2 * TOK and EC == 2 and HC == 8 and NT == 4 and NH % 2 == 0 and NH >= 6

    T_PRO, M_PRO, F_PRO = 17, 2 * NT, 2 * EC
    T_AT, M_AT, F_AT = [T_PRO], [M_PRO], [F_PRO]
    for n in range(NH + 1):
        near, late = n < NH - 2, n >= 1
        T_AT.append(T_AT[n] + NT + 2 * EC + NT + EC * (n < NH - 3) + NT + 2 * (n == 0))
        M_AT.append(M_AT[n] + (n >= 2) + NT * near + NT * (n < NH) + (NT - 1) * late)
        F_AT.append(F_AT[n] + EC * near + HC)
    T_PER, M_PER, F_PER = T_AT[3] - T_AT[2], M_AT[3] - M_AT[2], F_AT[3] - F_AT[2]
    assert (2 * T_PER) % 3 == 0 and M_PER % 2 == 0 and F_PER % 2 == 0

    def t_uses(h):
        return Uses(T_AT[h.n] + 2 * T_PER * h.lap, T_AT[h.n] % 3, 3)

    def m_uses(h):
        return Uses(M_AT[h.n] + 2 * M_PER * h.lap, M_AT[h.n] % 2, 2)

    def f_uses(h):
        return Uses(F_AT[h.n] + 2 * F_PER * h.lap, F_AT[h.n] % 2, 2)

    def after(eng, sem, count):
        if not isinstance(count, int) or count > 0:
            eng.wait_ge(sem, count)

    x_v = x.rearrange("b s e -> (b s) e").rearrange("(n p t) e -> p n t e", p=P, t=NT)
    out_v = out.rearrange("b s e -> (b s) e").rearrange("(n p t) e -> p n t e", p=P, t=NT)

    with ExitStack() as ctx:
        def sb(name, shape, dt=F32):
            return ctx.enter_context(nc.sbuf_tensor(name, shape, dt))

        def sem(name):
            return ctx.enter_context(nc.semaphore(name))

        T = [ctx.enter_context(nc.psum_tensor(f"T{i}", [P, 512], F32)) for i in range(3)]
        M = [ctx.enter_context(nc.psum_tensor(f"M{i}", [P, 512], F32)) for i in range(2)]
        F = [ctx.enter_context(nc.psum_tensor(f"F{i}", [P, 512], F32)) for i in range(2)]
        state = ctx.enter_context(nc.psum_tensor("state", [P, 512], F32))

        ident = sb("ident", [P, P])
        ones = sb("ones", [P, P])
        ones_r = sb("ones_r", [1, P], F32R)
        head_mask = sb("head_mask", [P, HB, HD])
        minus_half = sb("minus_half", [P, 2 * NT])

        wq_hi = sb("wq_hi", [P, EC, E], F32R)
        wq_lo = sb("wq_lo", [P, EC, E], F32R)
        wkv_hi = sb("wkv_hi", [P, EC, 2 * E], F32R)
        wkv_lo = sb("wkv_lo", [P, EC, 2 * E], F32R)
        wo_hi = sb("wo_hi", [P, EC, E], F32R)
        wo_lo = sb("wo_lo", [P, EC, E], F32R)
        w1_t = sb("w1_t", [P, EC, HID], F32R)
        w2_t = sb("w2_t", [P, HC, E], F32R)

        VEC = {"bq": (0, EC), "g1": (EC, EC), "c1": (2 * EC, EC), "b1": (3 * EC, HC),
               "g2": (3 * EC + HC, HC), "c2": (3 * EC + 2 * HC, HC)}
        NV = 3 * EC + 3 * HC
        vec_rows = sb("vec_rows", [NV, P])
        vec = sb("vec", [P, NV])
        bq_plus_1 = sb("bq_plus_1", [P, EC])
        minus_bq = sb("minus_bq", [P, EC])
        gc2 = sb("gc2", [P, HC, 2])
        gc2_hi = sb("gc2_hi", [P, HC, 2], F32R)
        gc2_lo = sb("gc2_lo", [P, HC, 2], F32R)
        c1_parts = sb("c1_parts", [P, EC, 2], F32R)
        b1_lo = sb("b1_lo", [P, HC])
        bk_row = sb("bk_row", [1, E])
        bk_hi = sb("bk_hi", [1, E], F32R)
        bk_lo = sb("bk_lo", [1, E], F32R)
        bv_all = sb("bv_all", [P, E])
        bo_all = sb("bo_all", [P, E])
        b2_all = sb("b2_all", [P, E])
        b1_all = sb("b1_all", [P, HC])
        ce_rows = sb("ce_rows", [2, E])
        pick = sb("pick", [2, 2, P])
        c_all = sb("c_all", [P, E])
        e_all = sb("e_all", [P, E])
        abs_part = sb("abs_part", [P, 2, HC])
        abs_sum = sb("abs_sum", [P, 2])
        mean_abs = sb("mean_abs", [P, 2])
        quant = sb("quant", [P, 2])
        step = sb("step", [P, 2])

        x_in = sb("x_in", [P, 2, NT, E])
        xt_hi = sb("xt_hi", [P, EC, TOK], F32R)
        xt_lo = sb("xt_lo", [P, EC, TOK], F32R)
        q_t = sb("q_t", [P, 2, EC, TOK])
        exp_k = sb("exp_k", [P, 2, E])
        k_sb = sb("k_sb", [P, NT, E])
        v_sb = sb("v_sb", [P, NT, EC, VW])
        k_sum = sb("k_sum", [P, EC, 1])
        kv_raw = sb("kv_raw", [P, EC, P])
        kv = sb("kv", [P, EC, AW])

        den = sb("den", [P, NT, HEADS])
        inv_den = sb("inv_den", [P, NT, HEADS])
        attn = sb("attn", [P, NT, E])
        at_hi = sb("at_hi", [P, EC, TOK], F32R)
        at_lo = sb("at_lo", [P, EC, TOK], F32R)
        x_bo = sb("x_bo", [P, 2, NT, E])
        y1 = sb("y1", [P, NT, E])
        z = sb("z", [P, NT, E])
        exp_q = z[:].rearrange("p t e -> p (t e)").rearrange("p (c s) -> p c s", c=EC)
        ht_hi, ht_lo = at_hi, at_lo
        g = sb("g", [P, HC, TOK])
        g_hi = sb("g_hi", [P, 2, HC, TOK], F32R)
        g_lo = sb("g_lo", [P, 2, HC, TOK], F32R)
        x1_e = sb("x1_e", [P, 2, NT, E])
        y2 = sb("y2", [P, 2, NT, E])
        st1 = sb("st1", [P, NT, 6])
        mv1 = sb("mv1", [P, NT, 2])
        var1 = sb("var1", [P, 2, NT])
        r1 = sb("r1", [P, 2, NT])
        st2 = sb("st2", [P, NT, 2, 6])
        mv2 = sb("mv2", [P, NT, 2])
        var2 = sb("var2", [P, NT])
        minus_mean2 = sb("minus_mean2", [P, NT])
        r2 = sb("r2", [P, NT])
        r2_step = sb("r2_step", [P, NT])
        st3 = sb("st3", [P, NT, 6])
        mv3 = sb("mv3", [P, NT, 2])
        var3 = sb("var3", [P, NT])
        r3 = sb("r3", [P, NT])
        mean_r1 = sb("mean_r1", [P, NT])
        shift1 = sb("shift1", [P, NT])
        mean_r3 = sb("mean_r3", [P, NT])
        shift3 = sb("shift3", [P, NT])
        minus_ones = sb("minus_ones", [P, NT])
        table = sb("table", [P, 2])

        unused = sb("unused", [P, 4])
        pool_unused = sb("pool_unused", [P, 1])

        w_raw = [y1, z, attn, y2[:, 0]]
        w1_raw, w2_raw = g[:, 0:4, :], g[:, 4:8, :]

        x_loaded = [sem("x_loaded_0"), sem("x_loaded_1")]
        w_loaded = [sem(f"w_loaded_{i}") for i in range(4)]
        ffn_loaded = [sem("w1_loaded"), sem("w2_loaded")]
        vec_loaded = sem("vec_loaded")
        rows_loaded = sem("rows_loaded")
        setup_made = sem("setup_made")
        prep = sem("prep")
        consts_made = sem("consts_made")
        w_hi_made = sem("w_hi_made")
        t_filled, t_drained = sem("t_filled"), sem("t_drained")
        m_filled, m_drained = sem("m_filled"), sem("m_drained")
        f_filled = sem("f_filled")
        x_hi_made = sem("x_hi_made")
        relu_q_made = sem("relu_q_made")
        relu_k_made = sem("relu_k_made")
        exp_q_made = sem("exp_q_made")
        q_made = sem("q_made")
        exp_k_made = sem("exp_k_made")
        state_summed = sem("state_summed")
        state_step = sem("state_step")
        kv_made = sem("kv_made")
        attn_step = sem("attn_step")
        a_hi_made = sem("a_hi_made")
        x_bo_made = sem("x_bo_made")
        ln1_step = sem("ln1_step")
        r1_made = sem("r1_made")
        x1_made = sem("x1_made")
        x1_e_made = sem("x1_e_made")
        z_made = sem("z_made")
        h_hi_made = sem("h_hi_made")
        gelu_made = sem("gelu_made")
        g_hi_made = sem("g_hi_made")
        g_lo_made = sem("g_lo_made")
        ln2_step = sem("ln2_step")
        r2_made = sem("r2_made")
        y2_made = sem("y2_made")
        ln3_step = sem("ln3_step")
        r3_made = sem("r3_made")
        out_made = sem("out_made")
        out_free = [sem("out_free_0"), sem("out_free_1")]

        def vcol(name, k):
            return vec[:, VEC[name][0] + k:VEC[name][0] + k + 1]

        def f32(ap):
            return ap.bitcast(F32)

        def load_vectors(eng, vectors):
            for name, v in vectors:
                at, n = VEC[name]
                eng.dma_start(vec_rows[at:at + n, :], v.rearrange("(c p) -> c p", p=P)).then_inc(vec_loaded, 16)

        block = ctx.enter_context(nc.Block())

        @block.sync
        def _(sp):
            def load_x(h):
                sp.dma_start(x_in[:, h.par], x_v[:, h.at(1)]).then_inc(x_loaded[h.par], 16)

            def load_w(i, w):
                sp.dma_start(w_raw[i][:, 0:EC, :], w.rearrange("(c p) e -> p c e", p=P)).then_inc(w_loaded[i], 16)

            load_w(0, Wq)
            load_x(Half(0))
            load_w(1, Wk)
            load_w(2, Wv)
            load_vectors(sp, (("b1", b1), ("g2", ln2_g), ("c2", ln2_b)))
            sp.dma_start(bk_row[:], bk.rearrange("(a e) -> a e", a=1)).then_inc(rows_loaded, 16)
            for dst, v in ((bv_all, bv), (bo_all, bo), (b2_all, b2)):
                sp.dma_start(dst[:], v.rearrange("(a e) -> a e", a=1).to_broadcast([P, E])).then_inc(rows_loaded, 16)
            sp.dma_start(w1_raw.rearrange("p a (b e) -> p (a b) e", e=E),
                         w1.rearrange("(j p) e -> p j e", p=P)).then_inc(ffn_loaded[0], 16)
            sp.dma_start(w2_raw.rearrange("p (c a) e -> p c (a e)", c=EC),
                         w2.rearrange("(c p) h -> p c h", p=P)).then_inc(ffn_loaded[1], 16)
            load_x(Half(1))
            load_w(3, Wo)

            for n in (0, 1):
                sp.wait_ge(t_filled, X_TURNED[n])
                sp.wait_ge(x_bo_made, n + 1)
                load_x(Half(n + 2))

            def half(h):
                if h.n + 4 < NH:
                    sp.wait_ge(t_filled, T_AT[h.n] + 2 * T_PER * h.lap)
                    sp.wait_ge(x_bo_made, h.at(1, 3))
                    load_x(h.ahead(4))
                if h.n >= 2:
                    store(h.ahead(-2))

            def store(h):
                sp.wait_ge(out_made, h.at(NT, NT))
                sp.dma_start(out_v[:, h.at(1)], y2[:, h.par]).then_inc(out_free[h.par], 16)

            half(Half(0))
            half(Half(1))
            with sp.Fori(0, LAPS) as lap:
                half(Half(2, lap))
                half(Half(3, lap))
            for n in TAIL:
                half(Half(n))
            store(Half(NH - 2))
            store(Half(NH - 1))
            for par in (0, 1):
                sp.wait_ge(out_free[par], 16 * (NH // 2 + 1))

        @block.gpsimd
        def _(pool):
            pool.memset(ident[:], 0.0).then_inc(setup_made, 1)
            pool.memset(head_mask[:], 1.0).then_inc(setup_made, 1)
            pool.wait_ge(setup_made, 2)
            pool.affine_select(out=ident[:], in_=ident[:], compare_op=ALU.not_equal, fill=1.0, base=0,
                               pattern=[[-1, P]], channel_multiplier=1).then_inc(setup_made, 1)
            pool.affine_select(out=head_mask[:], in_=head_mask[:], compare_op=ALU.is_ge, fill=0.0, base=0,
                               pattern=[[-HD, HB], [0, HD]], channel_multiplier=1).then_inc(setup_made, 1)
            pool.wait_ge(setup_made, 4)
            pool.affine_select(out=head_mask[:], in_=head_mask[:], compare_op=ALU.is_ge, fill=0.0, base=HD - 1,
                               pattern=[[HD, HB], [0, HD]], channel_multiplier=-1).then_inc(setup_made, 1)
            pool.memset(ones[:], 1.0).then_inc(setup_made, 1)
            pool.memset(f32(ones_r[:]), 1.0).then_inc(setup_made, 1)
            pool.memset(minus_half[:], -0.5).then_inc(setup_made, 1)
            pool.memset(minus_ones[:], -1.0).then_inc(setup_made, 1)
            pool.memset(v_sb[:], 1.0).then_inc(setup_made, 1)
            pool.wait_ge(setup_made, 10)

            def rows_plus_bo(h):
                pool.wait_ge(x_loaded[h.par], 16 * (h.n // 2 + 1) + 16 * h.lap)
                pool.tensor_tensor(x_bo[:, h.par], x_in[:, h.par], bo_all[:, None, :].to_broadcast([P, NT, E]),
                                   ALU.add).then_inc(x_bo_made, 1)

            pool.wait_ge(rows_loaded, 64)
            rows_plus_bo(Half(0))
            rows_plus_bo(Half(1))

            def carry_wait():
                pool.tensor_tensor(pool_unused[:], minus_ones[:, 0:1], minus_ones[:, 0:1], ALU.mult)

            def power2(h):
                pool.wait_ge(ln2_step, h.at(NT + 2, NT + 2))
                pool.tensor_tensor(r2[:], var2[:], minus_half[:, 0:NT], ALU.pow).then_inc(r2_made, 1)
                pool.wait_ge(r2_made, h.at(2, 1))
                pool.tensor_tensor(r2_step[:], r2[:], step[:, 1:2].to_broadcast([P, NT]), ALU.mult).then_inc(r2_made, 1)

            def power3(h):
                pool.wait_ge(ln3_step, h.at(2 * NT + 1, 2 * NT + 1))
                after(pool, out_made, h.at(NT))
                pool.tensor_tensor(r3[:], var3[:], minus_half[:, 0:NT], ALU.pow).then_inc(r3_made, 1)
                pool.wait_ge(r3_made, h.at(3, 1))
                pool.tensor_tensor(mean_r3[:], mv3[:, :, 0], r3[:], ALU.mult).then_inc(r3_made, 1)
                pool.wait_ge(r3_made, h.at(3, 2))
                pool.tensor_tensor(shift3[:], mean_r3[:], minus_ones[:], ALU.mult).then_inc(r3_made, 1)

            def make_out(h):
                pool.wait_ge(r3_made, h.at(3, 3))
                for t in range(NT):
                    if t == 0:
                        carry_wait()
                    pool.tensor_scalar(y2[:, h.par, t], y2[:, h.par, t], r3[:, t:t + 1], shift3[:, t:t + 1],
                                       ALU.mult, ALU.add).then_inc(out_made, 1)

            def half(h):
                pool.wait_ge(ln1_step, h.at(2 * NT + 2, 2 * NT + 2))
                pool.tensor_tensor(r1[:, 1], var1[:, 1], minus_half[:, 0:NT], ALU.pow).then_inc(r1_made, 1)
                pool.tensor_tensor(r1[:, 0], var1[:, 0], minus_half[:, 0:NT], ALU.pow).then_inc(r1_made, 1)
                pool.wait_ge(r1_made, h.at(4, 2))
                pool.tensor_tensor(mean_r1[:], mv1[:, :, 0], r1[:, 0], ALU.mult).then_inc(r1_made, 1)
                pool.wait_ge(r1_made, h.at(4, 3))
                pool.tensor_tensor(shift1[:], mean_r1[:], minus_ones[:], ALU.mult).then_inc(r1_made, 1)
                pool.wait_ge(r1_made, h.at(4, 4))
                if h.n >= 1:
                    power2(h.ahead(-1))
                if h.n < NH - 2:
                    rows_plus_bo(h.ahead(2))
                if h.n >= 2:
                    power3(h.ahead(-2))
                for t in range(NT):
                    pool.tensor_scalar(x1_e[:, h.par, t], y1[:, t], r1[:, 0, t:t + 1], shift1[:, t:t + 1],
                                       ALU.mult, ALU.add).then_inc(x1_made, 1)
                if h.n == 0:
                    pool.wait_ge(consts_made, 2)
                pool.wait_ge(x1_made, h.at(NT, NT))
                pool.tensor_tensor(x1_e[:, h.par], x1_e[:, h.par], e_all[:, None, :].to_broadcast([P, NT, E]),
                                   ALU.add).then_inc(x1_e_made, 1)
                if h.n >= 2:
                    make_out(h.ahead(-2))

            half(Half(0))
            half(Half(1))
            with pool.Fori(0, LAPS) as lap:
                half(Half(2, lap))
                half(Half(3, lap))
            for n in TAIL:
                half(Half(n))
            power2(Half(NH - 1))
            for n in (NH - 2, NH - 1):
                power3(Half(n))
                make_out(Half(n))

        @block.tensor
        def _(pe):
            def turn(tu, tiles):
                u, bank = tu.take()
                after(pe, t_drained, u - 2)
                for at, src in tiles:
                    mm = pe.transpose(T[bank][:, at * P:at * P + P], src, ident[:])
                mm.then_inc(t_filled, 1)

            def turn_x(h, tu):
                pe.wait_ge(x_loaded[h.par], 16 * (h.n // 2 + 1) + 16 * h.lap)
                for c in range(EC):
                    turn(tu, [(t, x_in[:, h.par, t, c * P:c * P + P]) for t in range(NT)])

            def project_q(h, c, fu):
                _, bank = fu.take()
                if h.n >= 3:
                    pe.wait_ge(gelu_made, h.ahead(-3).at(HC, HC - EC + c + 1))
                elif h.n >= 1:
                    pe.wait_ge(q_made, (h.n - 1) * EC + c + 1)
                k = 0
                for ec in range(EC):
                    for w, xt in ((wq_hi, xt_hi), (wq_hi, xt_lo), (wq_lo, xt_hi)):
                        mm = pe.matmul(F[bank][:], w[:, ec, c * P:c * P + P], xt[:, ec],
                                       start=(k == 0), stop=(k == 3 * EC - 1))
                        k += 1
                mm.then_inc(f_filled, 1)

            def project_kv(t, mu):
                u, bank = mu.take()
                after(pe, m_drained, u - 1)
                k = 0
                for ec in range(EC):
                    for xt, w in ((xt_hi, wkv_hi), (xt_lo, wkv_hi), (xt_hi, wkv_lo)):
                        pe.matmul(M[bank][:], xt[:, ec, t * P:t * P + P], w[:, ec], start=(k == 0), stop=False)
                        k += 1
                pe.matmul(M[bank][:, 0:E], ones_r[:], bk_hi[:], start=False, stop=False)
                pe.matmul(M[bank][:, 0:E], ones_r[:], bk_lo[:], start=False, stop=True).then_inc(m_filled, 1)

            def sum_state(h, kv_drained):
                if h.par == 0 and h.n >= 2:
                    pe.wait_ge(kv_made, (h.n // 2) * 2 * EC + 2 * EC * h.lap)
                pe.wait_ge(m_drained, kv_drained)
                for t in range(NT):
                    for c in range(EC):
                        first = h.par == 0 and t == 0
                        last = h.par == 1 and t == NT - 1
                        mm = pe.matmul(state[:, c * AW:c * AW + P + 1], k_sb[:, t, c * P:c * P + P],
                                       v_sb[:, t, c, 0:P + 1], start=first and c == 0, stop=last,
                                       skip_group_check=True)
                if h.par == 1:
                    mm.then_inc(state_summed, 1)

            def attend(h, t, tu):
                if t == 0:
                    pe.wait_ge(kv_made, (h.n // 2 + 1) * 2 * EC + 2 * EC * h.lap)
                    pe.wait_ge(q_made, h.at(EC, EC))
                u, bank = tu.take()
                pe.wait_ge(t_drained, u - 2)
                for c in range(EC):
                    mm = pe.matmul(T[bank][:, c * AW:c * AW + AW], q_t[:, h.par, c, t * P:t * P + P],
                                   kv[:, c], start=True, stop=True)
                mm.then_inc(t_filled, 1)

            def project_o(t, mu):
                u, bank = mu.take()
                pe.wait_ge(m_drained, u - 1)
                k = 0
                for ec in range(EC):
                    for a, w in ((at_hi, wo_hi), (at_lo, wo_hi), (at_hi, wo_lo)):
                        mm = pe.matmul(M[bank][:, 0:E], a[:, ec, t * P:t * P + P], w[:, ec],
                                       start=(k == 0), stop=(k == 3 * EC - 1))
                        k += 1
                mm.then_inc(m_filled, 1)

            def turn_gelu(h, part, t, tu):
                pe.wait_ge(gelu_made, h.at(HC, part * 4 + 4))
                turn(tu, [(i, g[:, part * 4 + i, t * P:t * P + P]) for i in range(4)])

            def feed_1(h, j, fu):
                _, bank = fu.take()
                if j >= EC:
                    pe.wait_ge(gelu_made, h.at(HC, j - 1))
                elif h.n < NH - 2:
                    pe.wait_ge(q_made, h.ahead(2).at(EC, j + 1))
                else:
                    pe.wait_ge(gelu_made, h.ahead(-1).at(HC, HC - EC + j + 1))
                k = 0
                for ec in range(EC):
                    for part in (ht_hi, ht_lo):
                        mm = pe.matmul(F[bank][:], w1_t[:, ec, j * P:j * P + P], part[:, ec],
                                       start=(k == 0), stop=(k == 2 * EC - 1))
                        k += 1
                mm.then_inc(f_filled, 1)

            def feed_2(h, t, mu):
                u, bank = mu.take()
                pe.wait_ge(g_lo_made, h.at(HC, HC))
                pe.wait_ge(m_drained, u - 1)
                for j in range(HC):
                    for part in (g_hi, g_lo):
                        mm = pe.matmul(M[bank][:, 0:E], part[:, h.par, j, t * P:t * P + P], w2_t[:, j],
                                       start=(j == 0 and part is g_hi), stop=(j == HC - 1 and part is g_lo))
                mm.then_inc(m_filled, 1)

            pe.wait_ge(setup_made, 10)
            tu, mu, fu = Uses(0, 0, 3), Uses(0, 0, 2), Uses(0, 0, 2)

            def turn_square(i):
                pe.wait_ge(w_loaded[i], 16)
                turn(tu, [(ec * EC + oc, w_raw[i][:, oc, ec * P:ec * P + P]) for ec in range(EC) for oc in range(EC)])

            w1_q = w1_raw.rearrange("p a (b e) -> p (a b) e", e=E)
            w2_q = w2_raw.rearrange("p (c a) e -> p c (a e)", c=EC)

            def turn_w1(ec, tu):
                for q in range(2):
                    turn(tu, [(i, w1_q[:, 4 * q + i, ec * P:ec * P + P]) for i in range(4)])

            def turn_w2(q, tu):
                turn(tu, [(i * EC + dc, w2_q[:, dc, (2 * q + i) * P:(2 * q + i) * P + P])
                          for i in range(2) for dc in range(EC)])

            turn_square(0)
            turn_x(Half(0), tu)
            x_turned = tu.k
            turn_square(1)
            turn_square(2)
            pe.wait_ge(vec_loaded, 6 * 16)
            u, bank = tu.take()
            pe.wait_ge(t_drained, u - 2)
            pe.transpose(T[bank][:, 0:NV], vec_rows[:], ident[0:NV, 0:NV]).then_inc(t_filled, 1)
            pe.wait_ge(t_drained, x_turned)
            for c in range(EC):
                project_q(Half(0), c, fu)
            pe.wait_ge(prep, PREP_BK)
            for t in range(NT):
                project_kv(t, mu)
            pe.wait_ge(prep, PREP_ABS)
            u, bank = tu.take()
            pe.wait_ge(t_drained, u - 2)
            pe.matmul(T[bank][:, 0:2], ones[:], abs_sum[:], start=True, stop=True).then_inc(t_filled, 1)
            turn_x(Half(1), tu)
            x_turned = tu.k
            sum_state(Half(0), NT)
            turn_square(3)
            pe.wait_ge(t_drained, x_turned)
            for c in range(EC):
                project_q(Half(1), c, fu)
            project_kv(0, mu)
            pe.wait_ge(prep, PREP_TERN1)
            turn_w1(0, tu)
            project_kv(1, mu)
            turn_w1(1, tu)
            project_kv(2, mu)
            project_kv(3, mu)
            turn_x(Half(2), tu)
            pe.wait_ge(prep, PREP_TERN2)
            u, bank = tu.take()
            pe.wait_ge(t_drained, u - 2)
            for j in range(HC):
                for ec in range(EC):
                    mm = pe.matmul(T[bank][:, 2 * j:2 * j + 2], w1_t[:, ec, j * P:j * P + P], c1_parts[:, ec],
                                   start=(ec == 0), stop=(ec == EC - 1))
            mm.then_inc(t_filled, 1)
            sum_state(Half(1), 2 * NT)
            assert tu.k == T_PRO and mu.k == M_PRO and fu.k == F_PRO

            def w2_times_rows(tu):
                u, bank = tu.take()
                pe.wait_ge(t_drained, u)
                for j in range(HC):
                    for part in (gc2_hi, gc2_lo):
                        mm = pe.matmul(T[bank][0:2, 0:E], part[:, j], w2_t[:, j],
                                       start=(j == 0 and part is gc2_hi), stop=(j == HC - 1 and part is gc2_lo))
                mm.then_inc(t_filled, 1)

            def spread_rows(tu):
                u, bank = tu.take()
                pe.wait_ge(t_drained, u)
                for i in range(2):
                    mm = pe.matmul(T[bank][:, i * E:i * E + E], pick[:, i], ce_rows[:], start=True, stop=True)
                mm.then_inc(t_filled, 1)

            def half(h):
                tu, mu, fu = t_uses(h), m_uses(h), f_uses(h)
                near, late = h.n < NH - 2, h.n >= 1
                if near:
                    pe.wait_ge(t_drained, tu.first - (NT if late else 0))
                    project_q(h.ahead(2), 0, fu)
                attend(h, 0, tu)
                attend(h, 1, tu)
                if h.n >= 2:
                    feed_2(h.ahead(-2), NT - 1, mu)
                attend(h, 2, tu)
                attend(h, 3, tu)
                attn_drained = tu.first + tu.k
                if near:
                    project_kv(0, mu)
                pe.wait_ge(t_drained, attn_drained)
                for c in range(EC):
                    turn(tu, [(t, attn[:, t, c * P:c * P + P]) for t in range(NT)])
                a_turned = tu.first + tu.k
                if near:
                    project_kv(1, mu)
                    project_q(h.ahead(2), 1, fu)
                if late:
                    turn_gelu(h.ahead(-1), 1, 0, tu)
                else:
                    pe.wait_ge(prep, PREP_TERN2)
                    turn_w2(0, tu)
                pe.wait_ge(t_drained, a_turned)
                for t in range(NT):
                    project_o(t, mu)
                for t in range(1, NT):
                    if late:
                        turn_gelu(h.ahead(-1), 1, t, tu)
                    else:
                        turn_w2(t, tu)
                if near:
                    for t in range(2, NT):
                        project_kv(t, mu)
                    kv_drained = mu.first + mu.k
                pe.wait_ge(z_made, h.at(NT, NT))
                for c in range(EC):
                    turn(tu, [(t, z[:, t, c * P:c * P + P]) for t in range(NT)])
                h_turned = tu.first + tu.k
                if late:
                    feed_2(h.ahead(-1), 0, mu)
                else:
                    w2_times_rows(tu)
                if near:
                    sum_state(h.ahead(2), kv_drained)
                pe.wait_ge(t_drained, h_turned)
                for j in range(HC):
                    feed_1(h, j, fu)
                    if late and j in FEED_2_AFTER:
                        feed_2(h.ahead(-1), 1 + FEED_2_AFTER.index(j), mu)
                    if h.n == 0 and j == 1:
                        spread_rows(tu)
                    if j == 2 and h.n < NH - 3:
                        turn_x(h.ahead(3), tu)
                    if j >= 4:
                        turn_gelu(h, 0, j - 4, tu)

            half(Half(0))
            half(Half(1))
            with pe.Fori(0, LAPS) as lap:
                half(Half(2, lap))
                half(Half(3, lap))
            for n in TAIL:
                half(Half(n))
            tu, mu = t_uses(Half(NH)), m_uses(Half(NH))
            feed_2(Half(NH - 2), NT - 1, mu)
            for t in range(NT):
                turn_gelu(Half(NH - 1), 1, t, tu)
            for t in range(NT):
                feed_2(Half(NH - 1), t, mu)

        @block.scalar
        def _(act):
            def hi_parts(sem_made, dst, tu, scale=None):
                for c in range(EC):
                    u, bank = tu.take()
                    act.wait_ge(t_filled, u + 1)
                    act.activation(dst[:, c], T[bank][:], ACT.Identity,
                                   scale=1.0 if scale is None else vcol(scale, c)).then_inc(sem_made, 1)

            def exps_q(h, c, fu):
                u, bank = fu.take()
                act.wait_ge(f_filled, u + 1)
                after(act, q_made, h.ahead(-1).at(EC, c + 1))
                act.activation(exp_q[:, c], F[bank][:], ACT.Relu, scale=-1.0,
                               bias=minus_bq[:, c:c + 1]).then_inc(relu_q_made, 1)
                act.wait_ge(relu_q_made, h.at(EC, c + 1))
                act.activation(exp_q[:, c], exp_q[:, c], ACT.Exp, scale=-1.0).then_inc(exp_q_made, 1)

            def keys_values(h, t, mu):
                u, bank = mu.take()
                act.wait_ge(m_filled, u + 1)
                act.activation(v_sb[:, t, :, 0:P], M[bank][:, E:2 * E].rearrange("p (c m) -> p c m", c=EC),
                               ACT.Identity)
                after(act, m_drained, u - 1)
                act.activation(exp_k[:, t % 2], M[bank][:, 0:E], ACT.Relu, scale=-1.0,
                               bias=ones[:, 0:1]).then_inc(relu_k_made, 1)
                act.wait_ge(relu_k_made, h.at(NT, t + 1))
                act.activation(exp_k[:, t % 2], exp_k[:, t % 2], ACT.Exp, scale=-1.0).then_inc(exp_k_made, 1)

            def make_g_hi(h, j):
                act.wait_ge(gelu_made, h.at(HC, j + 1))
                act.activation(g_hi[:, h.par, j], g[:, j], ACT.Identity, scale=vcol("g2", j)).then_inc(g_hi_made, 1)

            tu, mu, fu = Uses(0, 0, 3), Uses(0, 0, 2), Uses(0, 0, 2)

            def weight_hi(dst):
                u, bank = tu.take()
                act.wait_ge(t_filled, u + 1)
                act.activation(dst, T[bank][:].rearrange("p (c e) -> p c e", c=EC),
                               ACT.Identity).then_inc(w_hi_made, 1)

            load_vectors(act, (("bq", bq), ("g1", ln1_g), ("c1", ln1_b)))
            act.wait_ge(setup_made, 10)
            act.activation(table[:, 1:2], ones[:, 0:1], ACT.Exp)
            weight_hi(wq_hi[:])
            hi_parts(x_hi_made, xt_hi, tu)
            weight_hi(wkv_hi[:, :, 0:E])
            weight_hi(wkv_hi[:, :, E:2 * E])
            tu.take()
            act.wait_ge(prep, PREP_VEC)
            for c in range(EC):
                exps_q(Half(0), c, fu)
            for t in range(NT):
                keys_values(Half(0), t, mu)
            tu.take()
            hi_parts(x_hi_made, xt_hi, tu)
            weight_hi(wo_hi[:])
            for _ in range(4):
                tu.take()
            for c in range(EC):
                exps_q(Half(1), c, fu)
            for t in range(NT):
                keys_values(Half(1), t, mu)
            hi_parts(x_hi_made, xt_hi, tu)
            act.wait_ge(prep, PREP_END)

            def half(h):
                tu, mu, fu = t_uses(h), m_uses(h), f_uses(h)
                near, late = h.n < NH - 2, h.n >= 1
                for t in range(NT):
                    tu.take()
                if h.n >= 2:
                    mu.take()
                if near:
                    exps_q(h.ahead(2), 0, fu)
                    keys_values(h.ahead(2), 0, mu)
                hi_parts(a_hi_made, at_hi, tu)
                for t in range(NT):
                    tu.take()
                if near:
                    keys_values(h.ahead(2), 1, mu)
                    exps_q(h.ahead(2), 1, fu)
                for t in range(NT):
                    mu.take()
                if near:
                    keys_values(h.ahead(2), 2, mu)
                    keys_values(h.ahead(2), 3, mu)
                hi_parts(h_hi_made, ht_hi, tu, scale="g1")
                if h.n == 0:
                    for _ in range(2):
                        tu.take()
                act.activation(table[:, 0:1], ones[:, 0:1], ACT.Gelu)
                for j in range(HC):
                    u, bank = fu.take()
                    act.wait_ge(f_filled, u + 1)
                    if late and j % 4 == 0:
                        act.wait_ge(g_lo_made, h.ahead(-1).at(HC, j + 4))
                    act.activation(g[:, j], F[bank][:], ACT.Gelu, scale=step[:, 0:1],
                                   bias=b1_all[:, j:j + 1]).then_inc(gelu_made, 1)
                    if j >= 1:
                        make_g_hi(h, j - 1)
                    if j == 3 and h.n < NH - 3:
                        hi_parts(x_hi_made, xt_hi, tu)
                make_g_hi(h, HC - 1)
                if h.n < NH - 3:
                    act.activation(table[:, 1:2], ones[:, 0:1], ACT.Exp)

            half(Half(0))
            half(Half(1))
            with act.Fori(0, LAPS) as lap:
                half(Half(2, lap))
                half(Half(3, lap))
            for n in TAIL:
                half(Half(n))

        @block.vector
        def _(dve):
            def lo_parts(sem_made, made, hi, lo, tu, scale=None):
                for c in range(EC):
                    u, bank = tu.take()
                    dve.wait_ge(sem_made, made + c + 1)
                    if scale is None:
                        ins = dve.tensor_tensor(lo[:, c], T[bank][:], f32(hi[:, c]), ALU.subtract)
                    else:
                        ins = dve.scalar_tensor_tensor(lo[:, c], T[bank][:], vcol(scale, c), f32(hi[:, c]),
                                                       ALU.mult, ALU.subtract)
                    ins.then_inc(t_drained, 1)

            def make_q(h, c, fu):
                _, bank = fu.take()
                dve.wait_ge(exp_q_made, h.at(EC, c + 1))
                dve.scalar_tensor_tensor(q_t[:, h.par, c], F[bank][:], bq_plus_1[:, c:c + 1], exp_q[:, c],
                                         ALU.add, ALU.max).then_inc(q_made, 1)

            def make_k(h, t, mu):
                _, bank = mu.take()
                dve.wait_ge(exp_k_made, h.at(NT, t + 1))
                dve.tensor_tensor(k_sb[:, t], exp_k[:, t % 2], M[bank][:, 0:E], ALU.max).then_inc(m_drained, 1)

            def carry_wait():
                dve.memset(unused[:, 3:4], 0.0)

            def make_kv(h):
                done = (h.n // 2) + h.lap
                dve.wait_ge(state_summed, done + 1)
                sums = state[:, 0:EC * AW].rearrange("p (c w) -> p c w", c=EC)
                dve.tensor_copy(k_sum[:], sums[:, :, P:P + 1]).then_inc(state_step, 1)
                dve.wait_ge(state_step, 3 * done + 1)
                for c in range(EC):
                    dve.scalar_tensor_tensor(kv_raw[:, c], bv_all[:, c * P:c * P + P], k_sum[:, c],
                                             state[:, c * AW:c * AW + P], ALU.mult, ALU.add).then_inc(state_step, 1)
                dve.wait_ge(state_step, 3 * done + 3)
                for c in range(EC):
                    dve.tensor_tensor(kv[:, c, 0:P], kv_raw[:, c], head_mask[:].rearrange("p h m -> p (h m)"),
                                      ALU.mult).then_inc(kv_made, 1)
                    dve.tensor_scalar(kv[:, c, P:AW], head_mask[:, :, 0], k_sum[:, c], None,
                                      ALU.mult).then_inc(kv_made, 1)

            def attn_sums(bank):
                return T[bank][:, 0:EC * AW].rearrange("p (c w) -> p c w", c=EC)

            def make_attn(h, tu):
                for pair in range(0, NT, 2):
                    tiles = [(t, *tu.take()) for t in (pair, pair + 1)]
                    for t, u, bank in tiles:
                        dve.wait_ge(t_filled, u + 1)
                        dve.tensor_scalar(den[:, t].rearrange("p (c h) -> p c h", c=EC), attn_sums(bank)[:, :, P:AW],
                                          ATTN_EPS, None, ALU.add).then_inc(attn_step, 1)
                    for i, (t, u, bank) in enumerate(tiles):
                        dve.wait_ge(attn_step, h.at(2 * NT, 2 * pair + 1 + i))
                        dve.reciprocal(inv_den[:, t], den[:, t]).then_inc(attn_step, 1)
                    for i, (t, u, bank) in enumerate(tiles):
                        dve.wait_ge(attn_step, h.at(2 * NT, 2 * pair + 3 + i))
                        dve.tensor_tensor(attn[:, t].rearrange("p (c h m) -> p c h m", c=EC, h=HB),
                                          attn_sums(bank)[:, :, 0:P].rearrange("p c (h m) -> p c h m", h=HB),
                                          inv_den[:, t].rearrange("p (c h) -> p c h", c=EC)[:, :, :, None]
                                          .to_broadcast([P, EC, HB, HD]), ALU.mult).then_inc(t_drained, 1)

            def gelu_stats(part, t, tu):
                u, bank = tu.take()
                dve.wait_ge(t_filled, u + 1)
                dve.bn_stats(st2[:, t, part], T[bank][:]).then_inc(t_drained, 1)

            def gelu_moments(h, stats_drained):
                dve.wait_ge(t_drained, stats_drained)
                after(dve, r2_made, h.at(2, 0))
                carry_wait()
                for t in range(NT):
                    dve.bn_aggr(mv2[:, t], st2[:, t].rearrange("p a s -> p (a s)")).then_inc(ln2_step, 1)
                dve.wait_ge(ln2_step, h.at(NT + 2, NT))
                dve.tensor_scalar(var2[:], mv2[:, :, 1], LN_EPS, None, ALU.add).then_inc(ln2_step, 1)
                dve.tensor_scalar(minus_mean2[:], mv2[:, :, 0], -1.0, None, ALU.mult).then_inc(ln2_step, 1)

            def make_y1(h, mu):
                dve.wait_ge(x_bo_made, h.at(1, 1))
                after(dve, x1_made, h.at(NT, 0))
                for t in range(NT + 1):
                    if t < NT:
                        u, bank = mu.take()
                        dve.wait_ge(m_filled, u + 1)
                        dve.tensor_tensor(y1[:, t], M[bank][:, 0:E], x_bo[:, h.par, t], ALU.add).then_inc(m_drained, 1)
                    if t >= 1:
                        dve.wait_ge(m_drained, u if t < NT else u + 1)
                        dve.bn_stats(st1[:, t - 1], y1[:, t - 1]).then_inc(ln1_step, 1)
                dve.wait_ge(ln1_step, h.at(2 * NT + 2, NT))
                carry_wait()
                for t in range(NT):
                    dve.bn_aggr(mv1[:, t], st1[:, t]).then_inc(ln1_step, 1)
                dve.wait_ge(ln1_step, h.at(2 * NT + 2, 2 * NT))
                dve.tensor_scalar(var1[:, 0], mv1[:, :, 1], LN_EPS, None, ALU.add).then_inc(ln1_step, 1)
                dve.tensor_scalar(var1[:, 1], mv1[:, :, 1], 1.0 + LN_EPS, LN_EPS * LN_EPS, ALU.mult,
                                  ALU.add).then_inc(ln1_step, 1)

            def make_z(h):
                if h.n < NH - 2:
                    dve.wait_ge(q_made, h.ahead(2).at(EC, EC))
                dve.wait_ge(r1_made, h.at(4, 1))
                for t in range(NT):
                    dve.tensor_scalar(z[:, t], y1[:, t], mv1[:, t, 0:1], r1[:, 1, t:t + 1], ALU.subtract,
                                      ALU.mult).then_inc(z_made, 1)

            def drain_f(h, t, mu):
                u, bank = mu.take()
                if t == 0:
                    dve.wait_ge(ln2_step, h.at(NT + 2, NT + 2))
                    dve.wait_ge(out_free[h.par], 16 * (h.n // 2 + 1) + 16 * h.lap)
                dve.wait_ge(m_filled, u + 1)
                dve.scalar_tensor_tensor(y2[:, h.par, t], c_all[:], minus_mean2[:, t:t + 1], M[bank][:, 0:E],
                                         ALU.mult, ALU.add).then_inc(m_drained, 1)
                return u

            def make_y2(h, t, drained):
                if t == 0:
                    dve.wait_ge(r2_made, h.at(2, 2))
                    dve.wait_ge(x1_e_made, h.at(1, 1))
                dve.wait_ge(m_drained, drained + 1)
                dve.scalar_tensor_tensor(y2[:, h.par, t], y2[:, h.par, t], r2_step[:, t:t + 1], x1_e[:, h.par, t],
                                         ALU.mult, ALU.add).then_inc(y2_made, 1)

            def y2_moments(h):
                for t in range(NT):
                    dve.wait_ge(y2_made, h.at(NT, t + 1))
                    dve.bn_stats(st3[:, t], y2[:, h.par, t]).then_inc(ln3_step, 1)
                after(dve, r3_made, h.at(3, 0))
                dve.wait_ge(ln3_step, h.at(2 * NT + 1, NT))
                carry_wait()
                for t in range(NT):
                    dve.bn_aggr(mv3[:, t], st3[:, t]).then_inc(ln3_step, 1)
                dve.wait_ge(ln3_step, h.at(2 * NT + 1, 2 * NT))
                dve.tensor_scalar(var3[:], mv3[:, :, 1], LN_EPS, None, ALU.add).then_inc(ln3_step, 1)

            def make_g_lo(h, j):
                dve.wait_ge(g_hi_made, h.at(HC, j + 1))
                dve.scalar_tensor_tensor(g_lo[:, h.par, j], g[:, j], vcol("g2", j), f32(g_hi[:, h.par, j]), ALU.mult,
                                         ALU.subtract).then_inc(g_lo_made, 1)

            steps = [0]

            def done(ins):
                steps[0] += 1
                ins.then_inc(prep, 1)

            def settled():
                dve.wait_ge(prep, steps[0])

            tu, mu, fu = Uses(0, 0, 3), Uses(0, 0, 2), Uses(0, 0, 2)

            def weight_lo(n, hi, lo):
                u, bank = tu.take()
                dve.wait_ge(w_hi_made, n)
                dve.tensor_tensor(lo, T[bank][:].rearrange("p (c e) -> p c e", c=EC), f32(hi),
                                  ALU.subtract).then_inc(t_drained, 1)

            dve.wait_ge(setup_made, 10)
            weight_lo(1, wq_hi[:], wq_lo[:])
            lo_parts(x_hi_made, 0, xt_hi, xt_lo, tu)
            weight_lo(2, wkv_hi[:, :, 0:E], wkv_lo[:, :, 0:E])
            weight_lo(3, wkv_hi[:, :, E:2 * E], wkv_lo[:, :, E:2 * E])
            u, bank = tu.take()
            dve.wait_ge(t_filled, u + 1)
            dve.tensor_copy(vec[:], T[bank][:, 0:NV]).then_inc(t_drained, 1)
            dve.wait_ge(t_drained, u + 1)
            done(dve.tensor_scalar(bq_plus_1[:], vec[:, 0:EC], 1.0, None, ALU.add))
            done(dve.tensor_scalar(minus_bq[:], vec[:, 0:EC], -1.0, None, ALU.mult))
            done(dve.tensor_copy(gc2[:, :, 0], vec[:, VEC["g2"][0]:VEC["g2"][0] + HC]))
            done(dve.tensor_copy(gc2[:, :, 1], vec[:, VEC["c2"][0]:VEC["c2"][0] + HC]))
            dve.wait_ge(rows_loaded, 64)
            done(dve.tensor_scalar(bk_row[:], bk_row[:], 1.0, None, ALU.add))
            assert steps[0] == PREP_VEC
            settled()
            done(dve.tensor_copy(bk_hi[:], bk_row[:]))
            settled()
            done(dve.tensor_tensor(bk_lo[:], bk_row[:], f32(bk_hi[:]), ALU.subtract))
            assert steps[0] == PREP_BK

            def sum_abs(i, w, first, end):
                dve.wait_ge(ffn_loaded[i], 16)
                done(dve.tensor_reduce(abs_part[:, i, first:end],
                                       w.rearrange("p a (b e) -> p (a b) e", e=E)[:, first:end], AX.X, ALU.add,
                                       apply_absolute_value=True))

            def round_w(i, w):
                settled()
                done(dve.tensor_scalar(w, w, quant[:, i:i + 1], ROUND, ALU.mult, ALU.add))

            def clip_w(w):
                settled()
                done(dve.tensor_scalar(w, w, ROUND, 1.0, ALU.subtract, ALU.min))

            sum_abs(0, w1_raw, 0, HC)
            for c in range(EC):
                make_q(Half(0), c, fu)
            sum_abs(1, w2_raw, 0, HC // 2)
            make_k(Half(0), 0, mu)
            sum_abs(1, w2_raw, HC // 2, HC)
            make_k(Half(0), 1, mu)
            settled()
            done(dve.tensor_reduce(abs_sum[:], abs_part[:], AX.X, ALU.add))
            assert steps[0] == PREP_ABS
            make_k(Half(0), 2, mu)
            make_k(Half(0), 3, mu)
            u, bank = tu.take()
            dve.wait_ge(t_filled, u + 1)
            dve.tensor_scalar(mean_abs[:], T[bank][:, 0:2], 1.0 / (E * HID), SCALE_FLOOR, ALU.mult,
                              ALU.max).then_inc(t_drained, 1)
            dve.wait_ge(t_drained, u + 1)
            done(dve.reciprocal(quant[:], mean_abs[:]))
            settled()
            done(dve.reciprocal(step[:], quant[:]))
            lo_parts(x_hi_made, EC, xt_hi, xt_lo, tu)
            round_w(0, w1_raw)
            weight_lo(4, wo_hi[:], wo_lo[:])
            clip_w(w1_raw)
            assert steps[0] == PREP_TERN1

            def clip_w1(ec):
                for q in range(2):
                    u, bank = tu.take()
                    dve.wait_ge(t_filled, u + 1)
                    dve.tensor_scalar(w1_t[:, ec, q * 512:q * 512 + 512], T[bank][:], -1.0, None,
                                      ALU.max).then_inc(t_drained, 1)

            def clip_w2(q, tu):
                u, bank = tu.take()
                dve.wait_ge(t_filled, u + 1)
                dve.tensor_scalar(w2_t[:, 2 * q:2 * q + 2], T[bank][:].rearrange("p (i e) -> p i e", i=2), -1.0, None,
                                  ALU.max).then_inc(t_drained, 1)

            for c in range(EC):
                make_q(Half(1), c, fu)
            done(dve.tensor_copy(gc2_hi[:], gc2[:]))
            done(dve.tensor_copy(c1_parts[:, :, 0], vec[:, VEC["c1"][0]:VEC["c1"][0] + EC]))
            make_k(Half(1), 0, mu)
            clip_w1(0)
            round_w(1, w2_raw)
            make_k(Half(1), 1, mu)
            clip_w1(1)
            clip_w(w2_raw)
            make_k(Half(1), 2, mu)
            done(dve.tensor_tensor(gc2_lo[:], gc2[:], f32(gc2_hi[:]), ALU.subtract))
            done(dve.tensor_tensor(c1_parts[:, :, 1], vec[:, VEC["c1"][0]:VEC["c1"][0] + EC],
                                   f32(c1_parts[:, :, 0]), ALU.subtract))
            assert steps[0] == PREP_TERN2
            for i in range(2):
                done(dve.tensor_scalar(pick[:, i], ones[0:2, :], ident[0:2, i:i + 1], None, ALU.mult))
            for par in (0, 1):
                dve.memset(unused[:, par:par + 1], 0.0).then_inc(out_free[par], 16)
            make_k(Half(1), 3, mu)
            lo_parts(x_hi_made, 2 * EC, xt_hi, xt_lo, tu)
            u, bank = tu.take()
            dve.wait_ge(t_filled, u + 1)
            products = T[bank][:, 0:2 * HC].rearrange("p (j i) -> p j i", i=2)
            done(dve.scalar_tensor_tensor(b1_lo[:], products[:, :, 1], step[:, 0:1],
                                          vec[:, VEC["b1"][0]:VEC["b1"][0] + HC], ALU.mult, ALU.add))
            settled()
            dve.scalar_tensor_tensor(b1_all[:], products[:, :, 0], step[:, 0:1], b1_lo[:], ALU.mult,
                                     ALU.add).then_inc(t_drained, 1)
            dve.wait_ge(t_drained, u + 1)
            done(dve.memset(unused[:, 2:3], 0.0))
            assert steps[0] == PREP_END and tu.k == T_PRO
            make_kv(Half(1))

            def make_ce_rows(tu):
                u, bank = tu.take()
                dve.wait_ge(t_filled, u + 1)
                dve.tensor_copy(ce_rows[:], T[bank][0:2, 0:E]).then_inc(t_drained, 1)

            def make_ce(tu):
                u, bank = tu.take()
                dve.wait_ge(t_filled, u + 1)
                dve.tensor_copy(c_all[:], T[bank][:, 0:E]).then_inc(consts_made, 1)
                dve.scalar_tensor_tensor(e_all[:], T[bank][:, E:2 * E], step[:, 1:2], b2_all[:], ALU.mult,
                                         ALU.add).then_inc(consts_made, 1)
                dve.wait_ge(consts_made, 2)
                dve.memset(unused[:, 2:3], 0.0).then_inc(t_drained, 1)

            def half(h):
                tu, mu, fu = t_uses(h), m_uses(h), f_uses(h)
                near, late = h.n < NH - 2, h.n >= 1
                make_attn(h, tu)
                if h.n >= 2:
                    make_y2(h.ahead(-2), NT - 1, drain_f(h.ahead(-2), NT - 1, mu))
                if near:
                    make_q(h.ahead(2), 0, fu)
                    make_k(h.ahead(2), 0, mu)
                lo_parts(a_hi_made, h.at(EC), at_hi, at_lo, tu)
                if near:
                    make_k(h.ahead(2), 1, mu)
                if late:
                    gelu_stats(1, 0, tu)
                else:
                    clip_w2(0, tu)
                make_y1(h, mu)
                if near:
                    make_q(h.ahead(2), 1, fu)
                if late:
                    gelu_stats(1, 1, tu)
                else:
                    clip_w2(1, tu)
                make_z(h)
                for t in (2, 3):
                    if late:
                        gelu_stats(1, t, tu)
                    else:
                        clip_w2(t, tu)
                    if near:
                        make_k(h.ahead(2), t, mu)
                stats_drained = tu.first + tu.k
                lo_parts(h_hi_made, h.at(EC), ht_hi, ht_lo, tu, scale="g1")
                if h.n == 0:
                    make_ce_rows(tu)
                drained = []
                if late:
                    gelu_moments(h.ahead(-1), stats_drained)
                    drained.append(drain_f(h.ahead(-1), 0, mu))
                if h.n >= 2:
                    y2_moments(h.ahead(-2))
                if near and h.par == 1:
                    make_kv(h.ahead(2))
                for j in range(HC):
                    if j >= 4:
                        gelu_stats(0, j - 4, tu)
                    make_g_lo(h, j)
                    if h.n == 0 and j == 1:
                        make_ce(tu)
                    if late and j in FEED_2_AFTER:
                        t = 1 + FEED_2_AFTER.index(j)
                        drained.append(drain_f(h.ahead(-1), t, mu))
                        make_y2(h.ahead(-1), t - 1, drained[t - 1])
                    if j == 2 and h.n < NH - 3:
                        lo_parts(x_hi_made, h.ahead(3).at(EC), xt_hi, xt_lo, tu)
                    if late and j == FEED_2_AFTER[-1] + 1:
                        make_y2(h.ahead(-1), NT - 2, drained[NT - 2])

            half(Half(0))
            half(Half(1))
            with dve.Fori(0, LAPS) as lap:
                half(Half(2, lap))
                half(Half(3, lap))
            for n in TAIL:
                half(Half(n))
            last = Half(NH - 1)
            tu, mu = t_uses(Half(NH)), m_uses(Half(NH))
            make_y2(Half(NH - 2), NT - 1, drain_f(Half(NH - 2), NT - 1, mu))
            for t in range(NT):
                gelu_stats(1, t, tu)
            gelu_moments(last, tu.first + tu.k)
            drained = [drain_f(last, 0, mu)]
            for t in range(1, NT):
                drained.append(drain_f(last, t, mu))
                make_y2(last, t - 1, drained[t - 1])
            make_y2(last, NT - 1, drained[NT - 1])
            y2_moments(Half(NH - 2))
            y2_moments(last)


PREP_VEC = 5
PREP_BK = 7
PREP_ABS = 11
PREP_TERN1 = 15
PREP_TERN2 = 21
PREP_END = 25
X_TURNED = (3, 9)
ROUND = 1.5 * 2 ** 23
FEED_2_AFTER = (1, 3)
LAPS = 5
TAIL = (12, 13, 14, 15)

_INS = ['L0_attn_hidden_states', 'L0_attn_Wq', 'L0_attn_bq', 'L0_attn_Wk', 'L0_attn_bk', 'L0_attn_Wv', 'L0_attn_bv',
        'L0_attn_Wo', 'L0_attn_bo', 'L0_ffn_ln1_g', 'L0_ffn_ln1_b', 'L0_ffn_w1', 'L0_ffn_b1', 'L0_ffn_ln2_g',
        'L0_ffn_ln2_b', 'L0_ffn_w2', 'L0_ffn_b2']


def kernel(**inputs):
    import numpy as _np
    import concourse.bacc as _bacc
    from concourse import mybir as _mybir
    from concourse.bass_utils import run_bass_kernel_spmd as _run

    nc = _bacc.Bacc("TRN2", target_bir_lowering=False, num_devices=1)
    arrays, args = {}, []
    for name in _INS:
        a = _np.ascontiguousarray(inputs[name])
        arrays[f"in_{name}"] = a
        args.append(nc.dram_tensor(f"in_{name}", a.shape, _mybir.dt.from_np(a.dtype), kind="ExternalInput").ap())
    shape = inputs['L0_attn_hidden_states'].shape
    args.append(nc.dram_tensor("out_0", shape, _mybir.dt.float32, kind="ExternalOutput").ap())
    block_kernel(nc, *args)
    r = _run(nc, [arrays], core_ids=[0])
    return r.results[0]["out_0"]
```

```python
from contextlib import ExitStack

import concourse.bass as bass
from concourse import mybir

F32 = mybir.dt.float32
F32R = mybir.dt.float32r
ALU = mybir.AluOpType
ACT = mybir.ActivationFunctionType
AX = mybir.AxisListType

P = 128
ATTN_EPS = 1e-6
LN_EPS = 1e-5
SCALE_FLOOR = 1e-5


class Uses:

    def __init__(self, first, bank, banks):
        self.first, self.bank, self.banks, self.k = first, bank, banks, 0

    def take(self):
        k = self.k
        self.k += 1
        return self.first + k, (self.bank + k) % self.banks


class Half:

    def __init__(self, n, lap=0):
        self.n, self.lap, self.par = n, lap, n % 2

    def at(self, per_half, k=0):
        return per_half * self.n + k + 2 * per_half * self.lap

    def ahead(self, d):
        return Half(self.n + d, self.lap)


def block_kernel(nc, x, Wq, bq, Wk, bk, Wv, bv, Wo, bo, ln1_g, ln1_b, w1, b1, ln2_g, ln2_b, w2, b2, out):
    B, S, E = x.shape
    HID = w1.shape[0]
    HEADS = 16
    HD = E // HEADS
    TOK = 512
    NH = B * S // TOK
    NT = TOK // P
    EC = E // P
    HC = HID // P
    HB = P // HD
    AW = P + HB
    VW = P + 4
    assert S == 2 * TOK and EC == 2 and HC == 8 and NT == 4 and NH % 2 == 0 and NH >= 6

    T_PRO, M_PRO, F_PRO = 17, 2 * NT, 2 * EC
    T_AT, M_AT, F_AT = [T_PRO], [M_PRO], [F_PRO]
    for n in range(NH + 1):
        near, late = n < NH - 2, n >= 1
        T_AT.append(T_AT[n] + NT + 2 * EC + NT + EC * (n < NH - 3) + NT + 2 * (n == 0))
        M_AT.append(M_AT[n] + (n >= 2) + NT * near + NT * (n < NH) + (NT - 1) * late)
        F_AT.append(F_AT[n] + EC * near + HC)
    T_PER, M_PER, F_PER = T_AT[3] - T_AT[2], M_AT[3] - M_AT[2], F_AT[3] - F_AT[2]
    assert (2 * T_PER) % 3 == 0 and M_PER % 2 == 0 and F_PER % 2 == 0

    def t_uses(h):
        return Uses(T_AT[h.n] + 2 * T_PER * h.lap, T_AT[h.n] % 3, 3)

    def m_uses(h):
        return Uses(M_AT[h.n] + 2 * M_PER * h.lap, M_AT[h.n] % 2, 2)

    def f_uses(h):
        return Uses(F_AT[h.n] + 2 * F_PER * h.lap, F_AT[h.n] % 2, 2)

    def in_f_bank(h, t):
        return h.n == NH - 1 and t >= 2

    def after(eng, sem, count):
        if not isinstance(count, int) or count > 0:
            eng.wait_ge(sem, count)

    x_v = x.rearrange("b s e -> (b s) e").rearrange("(n p t) e -> p n t e", p=P, t=NT)
    out_v = out.rearrange("b s e -> (b s) e").rearrange("(n p t) e -> p n t e", p=P, t=NT)

    with ExitStack() as ctx:
        def sb(name, shape, dt=F32):
            return ctx.enter_context(nc.sbuf_tensor(name, shape, dt))

        def sem(name):
            return ctx.enter_context(nc.semaphore(name))

        T = [ctx.enter_context(nc.psum_tensor(f"T{i}", [P, 512], F32)) for i in range(3)]
        M = [ctx.enter_context(nc.psum_tensor(f"M{i}", [P, 512], F32)) for i in range(2)]
        F = [ctx.enter_context(nc.psum_tensor(f"F{i}", [P, 512], F32)) for i in range(2)]
        state = ctx.enter_context(nc.psum_tensor("state", [P, 512], F32))

        ident = sb("ident", [P, P])
        ones = sb("ones", [P, P])
        ones_r = sb("ones_r", [2, P], F32R)
        head_mask = sb("head_mask", [P, HB, HD])
        minus_half = sb("minus_half", [P, NT])

        wq_hi = sb("wq_hi", [P, EC, E], F32R)
        wq_lo = sb("wq_lo", [P, EC, E], F32R)
        wkv_hi = sb("wkv_hi", [P, EC, 2 * E], F32R)
        wkv_lo = sb("wkv_lo", [P, EC, 2 * E], F32R)
        wo_hi = sb("wo_hi", [P, EC, E], F32R)
        wo_lo = sb("wo_lo", [P, EC, E], F32R)
        w1_t = sb("w1_t", [P, EC, HID], F32R)
        w2_t = sb("w2_t", [P, HC, E], F32R)

        VEC = {"bq": (0, EC), "g1": (EC, EC), "c1": (2 * EC, EC), "b1": (3 * EC, HC),
               "g2": (3 * EC + HC, HC), "c2": (3 * EC + 2 * HC, HC)}
        NV = 3 * EC + 3 * HC
        vec = sb("vec", [P, NV])
        bq_plus_1 = sb("bq_plus_1", [P, EC])
        minus_bq = sb("minus_bq", [P, EC])
        gc2 = sb("gc2", [P, HC, 2])
        gc2_hi = sb("gc2_hi", [P, HC, 2], F32R)
        gc2_lo = sb("gc2_lo", [P, HC, 2], F32R)
        c1_parts = sb("c1_parts", [P, EC, 2], F32R)
        b1_lo = sb("b1_lo", [P, HC])
        bk_parts = sb("bk_parts", [2, E], F32R)
        bk_last = sb("bk_last", [2, E])
        row_sign = sb("row_sign", [2, 1])
        bv_all = sb("bv_all", [P, E])
        bo_all = sb("bo_all", [P, E])
        b2_all = sb("b2_all", [P, E])
        b1_all = sb("b1_all", [P, HC])
        ce_rows = sb("ce_rows", [2, E])
        pick = sb("pick", [2, 2, P])
        c_all = sb("c_all", [P, E])
        e_all = sb("e_all", [P, E])
        abs_part = sb("abs_part", [P, 2, HC])
        abs_sum = sb("abs_sum", [P, 2])
        mean_abs = sb("mean_abs", [P, 2])
        quant = sb("quant", [P, 2])
        step = sb("step", [P, 2])

        x_in = sb("x_in", [P, 2, NT, E])
        xt_hi = sb("xt_hi", [P, EC, TOK], F32R)
        xt_lo = sb("xt_lo", [P, EC, TOK], F32R)
        q_t = sb("q_t", [P, 2, EC, TOK])
        exp_k = sb("exp_k", [P, 2, E])
        k_sb = sb("k_sb", [P, NT, E])
        v_sb = sb("v_sb", [P, NT, EC, VW])
        k_sum = sb("k_sum", [P, EC, 1])
        kv_raw = sb("kv_raw", [P, EC, P])
        kv = sb("kv", [P, EC, AW])

        den = sb("den", [P, NT, HEADS])
        inv_den = sb("inv_den", [P, NT, HEADS])
        attn = sb("attn", [P, NT, E])
        at_hi = sb("at_hi", [P, EC, TOK], F32R)
        at_lo = sb("at_lo", [P, EC, TOK], F32R)
        x_bo = sb("x_bo", [P, 2, NT, E])
        y1 = sb("y1", [P, NT, E])
        z = sb("z", [P, NT, E])
        exp_q = z[:].rearrange("p t e -> p (t e)").rearrange("p (c s) -> p c s", c=EC)
        ht_hi, ht_lo = at_hi, at_lo
        g = sb("g", [P, HC, TOK])
        g_hi = sb("g_hi", [P, 2, HC, TOK], F32R)
        g_lo = sb("g_lo", [P, 2, HC, TOK], F32R)
        x1_e = sb("x1_e", [P, 2, NT, E])
        y2 = sb("y2", [P, 2, NT, E])
        st1 = sb("st1", [P, NT, 6])
        mv1 = sb("mv1", [P, NT, 2])
        var1 = sb("var1", [P, 2, NT])
        r1 = sb("r1", [P, 2, NT])
        st2 = sb("st2", [P, NT, 2, 6])
        mv2 = sb("mv2", [P, NT, 2])
        var2 = sb("var2", [P, NT])
        minus_mean2 = sb("minus_mean2", [P, NT])
        r2 = sb("r2", [P, NT])
        r2_step = sb("r2_step", [P, NT])
        shift2 = sb("shift2", [P, NT])
        mean_rows = sb("mean_rows", [P, 2, E])
        st3 = sb("st3", [P, NT, 6])
        mv3 = sb("mv3", [P, NT, 2])
        var3 = sb("var3", [P, NT])
        r3 = sb("r3", [P, NT])
        mean_r1 = sb("mean_r1", [P, NT])
        shift1 = sb("shift1", [P, NT])
        mean_r3 = sb("mean_r3", [P, NT])
        shift3 = sb("shift3", [P, NT])
        minus_ones = sb("minus_ones", [P, NT])
        table = sb("table", [P, 2])

        unused = sb("unused", [P, 4])
        pool_unused = sb("pool_unused", [P, 1])

        w_raw = [y1, z, attn, y2[:, 0]]
        vec_rows, bk_row = attn[0:NV, 2, 0:P], attn[0:2, 3, :]
        w1_raw, w2_raw = g[:, 0:4, :], g[:, 4:8, :]

        x_loaded = [sem("x_loaded_0"), sem("x_loaded_1")]
        w_loaded = [sem(f"w_loaded_{i}") for i in range(4)]
        ffn_loaded = [sem("w1_loaded"), sem("w2_loaded")]
        vec_loaded = sem("vec_loaded")
        rows_loaded = sem("rows_loaded")
        setup_made = sem("setup_made")
        prep = sem("prep")
        consts_made = sem("consts_made")
        w_hi_made = sem("w_hi_made")
        t_filled, t_drained = sem("t_filled"), sem("t_drained")
        m_filled, m_drained = sem("m_filled"), sem("m_drained")
        f_filled = sem("f_filled")
        x_hi_made = sem("x_hi_made")
        relu_q_made = sem("relu_q_made")
        relu_k_made = sem("relu_k_made")
        exp_q_made = sem("exp_q_made")
        q_made = sem("q_made")
        exp_k_made = sem("exp_k_made")
        state_summed = sem("state_summed")
        state_step = sem("state_step")
        kv_made = sem("kv_made")
        attn_step = sem("attn_step")
        a_hi_made = sem("a_hi_made")
        x_bo_made = sem("x_bo_made")
        ln1_step = sem("ln1_step")
        r1_made = sem("r1_made")
        x1_made = sem("x1_made")
        x1_e_made = sem("x1_e_made")
        mean_rows_made = sem("mean_rows_made")
        x1_c_made = sem("x1_c_made")
        z_made = sem("z_made")
        h_hi_made = sem("h_hi_made")
        gelu_made = sem("gelu_made")
        g_hi_made = sem("g_hi_made")
        g_lo_made = sem("g_lo_made")
        ln2_step = sem("ln2_step")
        r2_made = sem("r2_made")
        ln3_step = sem("ln3_step")
        r3_made = sem("r3_made")
        out_made = sem("out_made")
        last_out_made = [sem("last_out_made_0"), sem("last_out_made_1")]
        out_free = [sem("out_free_0"), sem("out_free_1")]

        def vcol(name, k):
            return vec[:, VEC[name][0] + k:VEC[name][0] + k + 1]

        def f32(ap):
            return ap.bitcast(F32)

        def load_vectors(eng, vectors):
            for name, v in vectors:
                at, n = VEC[name]
                eng.dma_start(vec_rows[at:at + n, :], v.rearrange("(c p) -> c p", p=P)).then_inc(vec_loaded, 16)

        block = ctx.enter_context(nc.Block())

        @block.sync
        def _(sp):
            def load_x(h):
                sp.dma_start(x_in[:, h.par], x_v[:, h.at(1)]).then_inc(x_loaded[h.par], 16)

            def load_w(i, w):
                sp.dma_start(w_raw[i][:, 0:EC, :], w.rearrange("(c p) e -> p c e", p=P)).then_inc(w_loaded[i], 16)

            load_w(0, Wq)
            load_x(Half(0))
            load_w(1, Wk)
            load_w(2, Wv)
            load_vectors(sp, (("b1", b1), ("g2", ln2_g), ("c2", ln2_b)))
            sp.dma_start(bk_row, bk.rearrange("(a e) -> a e", a=1).to_broadcast([2, E])).then_inc(rows_loaded, 16)
            for dst, v in ((bv_all, bv), (bo_all, bo), (b2_all, b2)):
                sp.dma_start(dst[:], v.rearrange("(a e) -> a e", a=1).to_broadcast([P, E])).then_inc(rows_loaded, 16)
            sp.dma_start(w1_raw.rearrange("p a (b e) -> p (a b) e", e=E),
                         w1.rearrange("(j p) e -> p j e", p=P)).then_inc(ffn_loaded[0], 16)
            sp.dma_start(w2_raw.rearrange("p (c a) e -> p c (a e)", c=EC),
                         w2.rearrange("(c p) h -> p c h", p=P)).then_inc(ffn_loaded[1], 16)
            load_x(Half(1))
            load_w(3, Wo)

            for n in (0, 1):
                sp.wait_ge(t_filled, X_TURNED[n])
                sp.wait_ge(x_bo_made, n + 1)
                load_x(Half(n + 2))

            def half(h):
                if h.n + 4 < NH:
                    sp.wait_ge(t_filled, T_AT[h.n] + 2 * T_PER * h.lap)
                    sp.wait_ge(x_bo_made, h.at(1, 3))
                    load_x(h.ahead(4))
                if h.n >= 2:
                    store(h.ahead(-2))

            def store(h):
                sp.wait_ge(out_made, h.at(NT, NT))
                sp.dma_start(out_v[:, h.at(1)], y2[:, h.par]).then_inc(out_free[h.par], 16)

            half(Half(0))
            half(Half(1))
            with sp.Fori(0, LAPS) as lap:
                half(Half(2, lap))
                half(Half(3, lap))
            for n in PEELED:
                half(Half(n))
            store(Half(NH - 4))
            store(Half(NH - 3))
            store(Half(NH - 2))
            last = Half(NH - 1)
            for i, t in enumerate((0, 2)):
                sp.wait_ge(last_out_made[i], 2)
                sp.dma_start(out_v[:, last.n, t:t + 2], y2[:, last.par, t:t + 2]).then_inc(out_free[last.par], 16)
            for par in (0, 1):
                sp.wait_ge(out_free[par], 16 * (NH // 2 + 1 + par))

        @block.gpsimd
        def _(pool):
            pool.memset(ident[:], 0.0).then_inc(setup_made, 1)
            pool.memset(head_mask[:], 1.0).then_inc(setup_made, 1)
            pool.wait_ge(setup_made, 2)
            pool.affine_select(out=ident[:], in_=ident[:], compare_op=ALU.not_equal, fill=1.0, base=0,
                               pattern=[[-1, P]], channel_multiplier=1).then_inc(setup_made, 1)
            pool.affine_select(out=head_mask[:], in_=head_mask[:], compare_op=ALU.is_ge, fill=0.0, base=0,
                               pattern=[[-HD, HB], [0, HD]], channel_multiplier=1).then_inc(setup_made, 1)
            pool.wait_ge(setup_made, 4)
            pool.affine_select(out=head_mask[:], in_=head_mask[:], compare_op=ALU.is_ge, fill=0.0, base=HD - 1,
                               pattern=[[HD, HB], [0, HD]], channel_multiplier=-1).then_inc(setup_made, 1)
            pool.memset(ones[:], 1.0).then_inc(setup_made, 1)
            pool.memset(f32(ones_r[:]), 1.0).then_inc(setup_made, 1)
            pool.memset(minus_half[:], -0.5).then_inc(setup_made, 1)
            pool.memset(minus_ones[:], -1.0).then_inc(setup_made, 1)
            pool.memset(v_sb[:], 1.0).then_inc(setup_made, 1)
            pool.wait_ge(setup_made, 10)

            def rows_plus_bo(h):
                pool.wait_ge(x_loaded[h.par], 16 * (h.n // 2 + 1) + 16 * h.lap)
                pool.tensor_tensor(x_bo[:, h.par], x_in[:, h.par], bo_all[:, None, :].to_broadcast([P, NT, E]),
                                   ALU.add).then_inc(x_bo_made, 1)

            pool.wait_ge(rows_loaded, 64)
            rows_plus_bo(Half(0))
            rows_plus_bo(Half(1))

            def carry_wait():
                pool.tensor_tensor(pool_unused[:], minus_ones[:, 0:1], minus_ones[:, 0:1], ALU.mult)

            def power2(h):
                pool.wait_ge(ln2_step, h.at(NT + 2, NT + 2))
                pool.tensor_tensor(r2[:], var2[:], minus_half[:], ALU.pow).then_inc(r2_made, 1)
                pool.wait_ge(r2_made, h.at(3, 1))
                pool.tensor_tensor(r2_step[:], r2[:], step[:, 1:2].to_broadcast([P, NT]), ALU.mult).then_inc(r2_made, 1)
                pool.wait_ge(r2_made, h.at(3, 2))
                pool.tensor_tensor(shift2[:], minus_mean2[:], r2_step[:], ALU.mult).then_inc(r2_made, 1)

            def take_mean2(h):
                for t in range(NT + 1):
                    if t < NT:
                        pool.wait_ge(r2_made, h.at(3, 3))
                        if t >= 2:
                            pool.wait_ge(x1_c_made, h.at(NT, t - 1))
                        pool.tensor_tensor(mean_rows[:, t % 2], c_all[:], shift2[:, t:t + 1].to_broadcast([P, E]),
                                           ALU.mult).then_inc(mean_rows_made, 1)
                    if t >= 1:
                        pool.wait_ge(mean_rows_made, h.at(NT, t))
                        pool.tensor_tensor(x1_e[:, h.par, t - 1], x1_e[:, h.par, t - 1], mean_rows[:, (t - 1) % 2],
                                           ALU.add).then_inc(x1_c_made, 1)

            def power3(h):
                pool.wait_ge(ln3_step, h.at(2 * NT + 1, 2 * NT + 1))
                after(pool, out_made, h.at(NT))
                pool.tensor_tensor(r3[:], var3[:], minus_half[:], ALU.pow).then_inc(r3_made, 1)
                pool.wait_ge(r3_made, h.at(3, 1))
                pool.tensor_tensor(mean_r3[:], mv3[:, :, 0], r3[:], ALU.mult).then_inc(r3_made, 1)
                pool.wait_ge(r3_made, h.at(3, 2))
                pool.tensor_tensor(shift3[:], mean_r3[:], minus_ones[:], ALU.mult).then_inc(r3_made, 1)

            def make_out(h):
                pool.wait_ge(r3_made, h.at(3, 3))
                for t in range(NT):
                    if t == 0:
                        carry_wait()
                    pool.tensor_scalar(y2[:, h.par, t], y2[:, h.par, t], r3[:, t:t + 1], shift3[:, t:t + 1],
                                       ALU.mult, ALU.add).then_inc(out_made, 1)

            def power1(h):
                pool.wait_ge(ln1_step, h.at(2 * NT + 2, 2 * NT + 2))
                pool.tensor_tensor(r1[:, 1], var1[:, 1], minus_half[:], ALU.pow).then_inc(r1_made, 1)
                pool.tensor_tensor(r1[:, 0], var1[:, 0], minus_half[:], ALU.pow).then_inc(r1_made, 1)
                pool.wait_ge(r1_made, h.at(4, 2))
                pool.tensor_tensor(mean_r1[:], mv1[:, :, 0], r1[:, 0], ALU.mult).then_inc(r1_made, 1)
                pool.wait_ge(r1_made, h.at(4, 3))
                pool.tensor_tensor(shift1[:], mean_r1[:], minus_ones[:], ALU.mult).then_inc(r1_made, 1)

            def first_rows(h):
                for t in range(NT):
                    pool.tensor_scalar(x1_e[:, h.par, t], y1[:, t], r1[:, 0, t:t + 1], shift1[:, t:t + 1],
                                       ALU.mult, ALU.add).then_inc(x1_made, 1)
                if h.n == 0:
                    pool.wait_ge(consts_made, 2)
                pool.wait_ge(x1_made, h.at(NT, NT))
                pool.tensor_tensor(x1_e[:, h.par], x1_e[:, h.par], e_all[:, None, :].to_broadcast([P, NT, E]),
                                   ALU.add).then_inc(x1_e_made, 1)

            def half(h):
                power1(h)
                pool.wait_ge(r1_made, h.at(4, 4))
                if h.n >= 1:
                    power2(h.ahead(-1))
                    pool.wait_ge(x1_e_made, h.at(1, 0))
                    take_mean2(h.ahead(-1))
                rows_plus_bo(h.ahead(2))
                if h.n >= 2:
                    power3(h.ahead(-2))
                first_rows(h)
                if h.n >= 2:
                    make_out(h.ahead(-2))

            half(Half(0))
            half(Half(1))
            with pool.Fori(0, LAPS) as lap:
                half(Half(2, lap))
                half(Half(3, lap))
            for n in PEELED:
                half(Half(n))

            a, b = Half(NH - 2), Half(NH - 1)
            pool.wait_ge(x1_e_made, a.n)
            power2(a.ahead(-1))
            take_mean2(a.ahead(-1))
            power1(a)
            pool.wait_ge(r1_made, a.at(4, 4))
            first_rows(a)
            power1(b)
            pool.wait_ge(r1_made, b.at(4, 4))
            first_rows(b)
            power3(a.ahead(-2))
            make_out(a.ahead(-2))
            power2(a)
            take_mean2(a)
            power3(b.ahead(-2))
            make_out(b.ahead(-2))
            pool.wait_ge(x1_e_made, NH)
            power2(b)
            power3(a)
            power3(b)

        @block.tensor
        def _(pe):
            def turn(tu, tiles):
                u, bank = tu.take()
                after(pe, t_drained, u - 2)
                for at, src in tiles:
                    mm = pe.transpose(T[bank][:, at * P:at * P + P], src, ident[:])
                mm.then_inc(t_filled, 1)

            def turn_x(h, tu):
                pe.wait_ge(x_loaded[h.par], 16 * (h.n // 2 + 1) + 16 * h.lap)
                for c in range(EC):
                    turn(tu, [(t, x_in[:, h.par, t, c * P:c * P + P]) for t in range(NT)])

            def project_q(h, c, fu):
                _, bank = fu.take()
                if h.n >= 3:
                    pe.wait_ge(gelu_made, h.ahead(-3).at(HC, HC - EC + c + 1))
                elif h.n >= 1:
                    pe.wait_ge(q_made, (h.n - 1) * EC + c + 1)
                k = 0
                for ec in range(EC):
                    for w, xt in ((wq_hi, xt_hi), (wq_hi, xt_lo), (wq_lo, xt_hi)):
                        mm = pe.matmul(F[bank][:], w[:, ec, c * P:c * P + P], xt[:, ec],
                                       start=(k == 0), stop=(k == 3 * EC - 1))
                        k += 1
                mm.then_inc(f_filled, 1)

            def project_kv(t, mu):
                u, bank = mu.take()
                after(pe, m_drained, u - 1)
                k = 0
                for ec in range(EC):
                    for xt, w in ((xt_hi, wkv_hi), (xt_lo, wkv_hi), (xt_hi, wkv_lo)):
                        pe.matmul(M[bank][:], xt[:, ec, t * P:t * P + P], w[:, ec], start=(k == 0), stop=False)
                        k += 1
                pe.matmul(M[bank][:, 0:E], ones_r[:], bk_parts[:], start=False, stop=True).then_inc(m_filled, 1)

            def sum_state(h, kv_drained):
                if h.par == 0 and h.n >= 2:
                    pe.wait_ge(kv_made, (h.n // 2) * 2 * EC + 2 * EC * h.lap)
                pe.wait_ge(m_drained, kv_drained)
                for t in range(NT):
                    for c in range(EC):
                        first = h.par == 0 and t == 0
                        last = h.par == 1 and t == NT - 1
                        mm = pe.matmul(state[:, c * AW:c * AW + P + 1], k_sb[:, t, c * P:c * P + P],
                                       v_sb[:, t, c, 0:P + 1], start=first and c == 0, stop=last,
                                       skip_group_check=True)
                if h.par == 1:
                    mm.then_inc(state_summed, 1)

            def attend(h, t, tu):
                if t == 0:
                    pe.wait_ge(kv_made, (h.n // 2 + 1) * 2 * EC + 2 * EC * h.lap)
                    pe.wait_ge(q_made, h.at(EC, EC))
                u, bank = tu.take()
                pe.wait_ge(t_drained, u - 2)
                for c in range(EC):
                    mm = pe.matmul(T[bank][:, c * AW:c * AW + AW], q_t[:, h.par, c, t * P:t * P + P],
                                   kv[:, c], start=True, stop=True)
                mm.then_inc(t_filled, 1)

            def project_o(t, mu, at_hi=at_hi, at_lo=at_lo):
                u, bank = mu.take()
                pe.wait_ge(m_drained, u - 1)
                k = 0
                for ec in range(EC):
                    for a, w in ((at_hi, wo_hi), (at_lo, wo_hi), (at_hi, wo_lo)):
                        mm = pe.matmul(M[bank][:, 0:E], a[:, ec, t * P:t * P + P], w[:, ec],
                                       start=(k == 0), stop=(k == 3 * EC - 1))
                        k += 1
                mm.then_inc(m_filled, 1)

            def turn_gelu(h, part, t, tu):
                pe.wait_ge(gelu_made, h.at(HC, part * 4 + 4))
                turn(tu, [(i, g[:, part * 4 + i, t * P:t * P + P]) for i in range(4)])

            def feed_1(h, j, fu):
                _, bank = fu.take()
                if j >= EC:
                    pe.wait_ge(gelu_made, h.at(HC, j - 1))
                elif h.n < NH - 2:
                    pe.wait_ge(q_made, h.ahead(2).at(EC, j + 1))
                else:
                    pe.wait_ge(gelu_made, h.ahead(-1).at(HC, HC - EC + j + 1))
                k = 0
                for ec in range(EC):
                    for part in (ht_hi, ht_lo):
                        mm = pe.matmul(F[bank][:], w1_t[:, ec, j * P:j * P + P], part[:, ec],
                                       start=(k == 0), stop=(k == 2 * EC - 1))
                        k += 1
                mm.then_inc(f_filled, 1)

            def feed_2(h, t, mu):
                u, bank = mu.take()
                if h.n < NH - 1:
                    pe.wait_ge(g_lo_made, h.at(HC, HC))
                if in_f_bank(h, t):
                    pe.wait_ge(gelu_made, h.at(HC, HC))
                else:
                    pe.wait_ge(m_drained, u - 1)
                rows = F[t % 2] if in_f_bank(h, t) else M[bank]
                for j in range(HC):
                    if h.n == NH - 1:
                        pe.wait_ge(g_lo_made, h.at(HC, j + 1))
                    for part in (g_hi, g_lo):
                        mm = pe.matmul(rows[:, 0:E], part[:, h.par, j, t * P:t * P + P], w2_t[:, j],
                                       start=(j == 0 and part is g_hi), stop=(j == HC - 1 and part is g_lo))
                mm.then_inc(m_filled, 1)

            pe.wait_ge(setup_made, 10)
            tu, mu, fu = Uses(0, 0, 3), Uses(0, 0, 2), Uses(0, 0, 2)

            def turn_square(i):
                pe.wait_ge(w_loaded[i], 16)
                turn(tu, [(ec * EC + oc, w_raw[i][:, oc, ec * P:ec * P + P]) for ec in range(EC) for oc in range(EC)])

            w1_q = w1_raw.rearrange("p a (b e) -> p (a b) e", e=E)
            w2_q = w2_raw.rearrange("p (c a) e -> p c (a e)", c=EC)

            def turn_w1(ec, tu):
                for q in range(2):
                    turn(tu, [(i, w1_q[:, 4 * q + i, ec * P:ec * P + P]) for i in range(4)])

            def turn_w2(q, tu):
                turn(tu, [(i * EC + dc, w2_q[:, dc, (2 * q + i) * P:(2 * q + i) * P + P])
                          for i in range(2) for dc in range(EC)])

            turn_square(0)
            turn_x(Half(0), tu)
            x_turned = tu.k
            turn_square(1)
            turn_square(2)
            pe.wait_ge(vec_loaded, 6 * 16)
            u, bank = tu.take()
            pe.wait_ge(t_drained, u - 2)
            pe.transpose(T[bank][:, 0:NV], vec_rows, ident[0:NV, 0:NV]).then_inc(t_filled, 1)
            pe.wait_ge(t_drained, x_turned)
            for c in range(EC):
                project_q(Half(0), c, fu)
            pe.wait_ge(prep, PREP_BK)
            for t in range(NT):
                project_kv(t, mu)
            pe.wait_ge(prep, PREP_ABS)
            u, bank = tu.take()
            pe.wait_ge(t_drained, u - 2)
            pe.matmul(T[bank][:, 0:2], ones[:], abs_sum[:], start=True, stop=True).then_inc(t_filled, 1)
            turn_x(Half(1), tu)
            x_turned = tu.k
            sum_state(Half(0), NT)
            turn_square(3)
            pe.wait_ge(t_drained, x_turned)
            for c in range(EC):
                project_q(Half(1), c, fu)
            project_kv(0, mu)
            pe.wait_ge(prep, PREP_TERN1)
            turn_w1(0, tu)
            project_kv(1, mu)
            turn_w1(1, tu)
            project_kv(2, mu)
            project_kv(3, mu)
            turn_x(Half(2), tu)
            pe.wait_ge(prep, PREP_TERN2)
            u, bank = tu.take()
            pe.wait_ge(t_drained, u - 2)
            for j in range(HC):
                for ec in range(EC):
                    mm = pe.matmul(T[bank][:, 2 * j:2 * j + 2], w1_t[:, ec, j * P:j * P + P], c1_parts[:, ec],
                                   start=(ec == 0), stop=(ec == EC - 1))
            mm.then_inc(t_filled, 1)
            sum_state(Half(1), 2 * NT)
            assert tu.k == T_PRO and mu.k == M_PRO and fu.k == F_PRO

            def w2_times_rows(tu):
                u, bank = tu.take()
                pe.wait_ge(t_drained, u)
                for j in range(HC):
                    for part in (gc2_hi, gc2_lo):
                        mm = pe.matmul(T[bank][0:2, 0:E], part[:, j], w2_t[:, j],
                                       start=(j == 0 and part is gc2_hi), stop=(j == HC - 1 and part is gc2_lo))
                mm.then_inc(t_filled, 1)

            def spread_rows(tu):
                u, bank = tu.take()
                pe.wait_ge(t_drained, u)
                for i in range(2):
                    mm = pe.matmul(T[bank][:, i * E:i * E + E], pick[:, i], ce_rows[:], start=True, stop=True)
                mm.then_inc(t_filled, 1)

            def half(h):
                tu, mu, fu = t_uses(h), m_uses(h), f_uses(h)
                near, late = h.n < NH - 2, h.n >= 1
                if near:
                    pe.wait_ge(t_drained, tu.first - (NT if late else 0))
                    project_q(h.ahead(2), 0, fu)
                attend(h, 0, tu)
                attend(h, 1, tu)
                if h.n >= 2:
                    feed_2(h.ahead(-2), NT - 1, mu)
                attend(h, 2, tu)
                attend(h, 3, tu)
                attn_drained = tu.first + tu.k
                if near:
                    project_kv(0, mu)
                pe.wait_ge(t_drained, attn_drained)
                for c in range(EC):
                    turn(tu, [(t, attn[:, t, c * P:c * P + P]) for t in range(NT)])
                a_turned = tu.first + tu.k
                if near:
                    project_kv(1, mu)
                    project_q(h.ahead(2), 1, fu)
                if late:
                    turn_gelu(h.ahead(-1), 1, 0, tu)
                else:
                    pe.wait_ge(prep, PREP_TERN2)
                    turn_w2(0, tu)
                pe.wait_ge(t_drained, a_turned)
                for t in range(NT):
                    project_o(t, mu)
                for t in range(1, NT):
                    if late:
                        turn_gelu(h.ahead(-1), 1, t, tu)
                    else:
                        turn_w2(t, tu)
                if near:
                    for t in range(2, NT):
                        project_kv(t, mu)
                    kv_drained = mu.first + mu.k
                pe.wait_ge(z_made, h.at(NT, NT))
                for c in range(EC):
                    turn(tu, [(t, z[:, t, c * P:c * P + P]) for t in range(NT)])
                h_turned = tu.first + tu.k
                if late:
                    feed_2(h.ahead(-1), 0, mu)
                else:
                    w2_times_rows(tu)
                if near:
                    sum_state(h.ahead(2), kv_drained)
                pe.wait_ge(t_drained, h_turned)
                for j in range(HC):
                    feed_1(h, j, fu)
                    if late and j in FEED_2_AFTER:
                        feed_2(h.ahead(-1), 1 + FEED_2_AFTER.index(j), mu)
                    if h.n == 0 and j == 1:
                        spread_rows(tu)
                    if j == 2 and h.n < NH - 3:
                        turn_x(h.ahead(3), tu)
                    if j >= 4:
                        turn_gelu(h, 0, j - 4, tu)

            half(Half(0))
            half(Half(1))
            with pe.Fori(0, LAPS) as lap:
                half(Half(2, lap))
                half(Half(3, lap))
            for n in PEELED:
                half(Half(n))

            a, b = Half(NH - 2), Half(NH - 1)
            tu, mu, fu = t_uses(a), m_uses(a), f_uses(a)

            def turn_attn(tu):
                pe.wait_ge(t_drained, tu.first + tu.k)
                for c in range(EC):
                    turn(tu, [(t, attn[:, t, c * P:c * P + P]) for t in range(NT)])
                return tu.first + tu.k

            def turn_z(h, tu):
                pe.wait_ge(z_made, h.at(NT, NT))
                for c in range(EC):
                    turn(tu, [(t, z[:, t, c * P:c * P + P]) for t in range(NT)])
                return tu.first + tu.k

            feed_2(a.ahead(-2), NT - 1, mu)
            for t in range(NT):
                turn_gelu(a.ahead(-1), 1, t, tu)
            attend(a, 0, tu)
            attend(a, 1, tu)
            feed_2(a.ahead(-1), 0, mu)
            attend(a, 2, tu)
            attend(a, 3, tu)
            feed_2(a.ahead(-1), 1, mu)
            a_turned = turn_attn(tu)
            feed_2(a.ahead(-1), 2, mu)
            pe.wait_ge(t_drained, a_turned)
            for t in range(NT):
                project_o(t, mu)
            attend(b, 0, tu)
            attend(b, 1, tu)
            feed_2(a.ahead(-1), 3, mu)
            h_turned = turn_z(a, tu)
            attend(b, 2, tu)
            attend(b, 3, tu)
            b_attended = tu.first + tu.k
            pe.wait_ge(t_drained, h_turned)
            for j in range(HC):
                feed_1(a, j, fu)
                if j == 0:
                    a_turned = turn_attn(tu)
                if j == 3:
                    pe.wait_ge(t_drained, a_turned)
                    for t in range(NT):
                        project_o(t, mu, xt_hi, xt_lo)
                if j >= 4:
                    turn_gelu(a, 0, j - 4, tu)
            h_turned = turn_z(b, tu)
            feed_2(a, 0, mu)
            turn_gelu(a, 1, 0, tu)
            turn_gelu(a, 1, 1, tu)
            pe.wait_ge(t_drained, h_turned)
            for j in range(HC):
                feed_1(b, j, fu)
                if j < 2:
                    turn_gelu(a, 1, 2 + j, tu)
                if j == 2:
                    feed_2(a, 1, mu)
                if j >= 4:
                    turn_gelu(b, 0, j - 4, tu)
            feed_2(a, 2, mu)
            turn_gelu(b, 1, 0, tu)
            turn_gelu(b, 1, 1, tu)
            feed_2(a, 3, mu)
            turn_gelu(b, 1, 2, tu)
            turn_gelu(b, 1, 3, tu)
            for t in range(NT):
                feed_2(b, t, mu)

        @block.scalar
        def _(act):
            def hi_parts(sem_made, dst, tu, scale=None):
                for c in range(EC):
                    u, bank = tu.take()
                    act.wait_ge(t_filled, u + 1)
                    act.activation(dst[:, c], T[bank][:], ACT.Identity,
                                   scale=1.0 if scale is None else vcol(scale, c)).then_inc(sem_made, 1)

            def exps_q(h, c, fu):
                u, bank = fu.take()
                act.wait_ge(f_filled, u + 1)
                after(act, q_made, h.ahead(-1).at(EC, c + 1))
                act.activation(exp_q[:, c], F[bank][:], ACT.Relu, scale=-1.0,
                               bias=minus_bq[:, c:c + 1]).then_inc(relu_q_made, 1)
                act.wait_ge(relu_q_made, h.at(EC, c + 1))
                act.activation(exp_q[:, c], exp_q[:, c], ACT.Exp, scale=-1.0).then_inc(exp_q_made, 1)

            def keys_values(h, t, mu):
                u, bank = mu.take()
                act.wait_ge(m_filled, u + 1)
                act.activation(v_sb[:, t, :, 0:P], M[bank][:, E:2 * E].rearrange("p (c m) -> p c m", c=EC),
                               ACT.Identity)
                after(act, m_drained, u - 1)
                act.activation(exp_k[:, t % 2], M[bank][:, 0:E], ACT.Relu, scale=-1.0,
                               bias=ones[:, 0:1]).then_inc(relu_k_made, 1)
                act.wait_ge(relu_k_made, h.at(NT, t + 1))
                act.activation(exp_k[:, t % 2], exp_k[:, t % 2], ACT.Exp, scale=-1.0).then_inc(exp_k_made, 1)

            def make_gelu(h, j, fu):
                u, bank = fu.take()
                act.wait_ge(f_filled, u + 1)
                if h.n >= 1 and j % 4 == 0:
                    act.wait_ge(g_lo_made, h.ahead(-1).at(HC, j + 4))
                act.activation(g[:, j], F[bank][:], ACT.Gelu, scale=step[:, 0:1],
                               bias=b1_all[:, j:j + 1]).then_inc(gelu_made, 1)

            def make_g_hi(h, j):
                act.wait_ge(gelu_made, h.at(HC, j + 1))
                act.activation(g_hi[:, h.par, j], g[:, j], ACT.Identity, scale=vcol("g2", j)).then_inc(g_hi_made, 1)

            tu, mu, fu = Uses(0, 0, 3), Uses(0, 0, 2), Uses(0, 0, 2)

            def weight_hi(dst):
                u, bank = tu.take()
                act.wait_ge(t_filled, u + 1)
                act.activation(dst, T[bank][:].rearrange("p (c e) -> p c e", c=EC),
                               ACT.Identity).then_inc(w_hi_made, 1)

            load_vectors(act, (("bq", bq), ("g1", ln1_g), ("c1", ln1_b)))
            act.wait_ge(setup_made, 10)
            act.activation(table[:, 1:2], ones[:, 0:1], ACT.Exp)
            weight_hi(wq_hi[:])
            hi_parts(x_hi_made, xt_hi, tu)
            weight_hi(wkv_hi[:, :, 0:E])
            weight_hi(wkv_hi[:, :, E:2 * E])
            tu.take()
            act.wait_ge(prep, PREP_VEC)
            for c in range(EC):
                exps_q(Half(0), c, fu)
            for t in range(NT):
                keys_values(Half(0), t, mu)
            tu.take()
            hi_parts(x_hi_made, xt_hi, tu)
            weight_hi(wo_hi[:])
            for _ in range(4):
                tu.take()
            for c in range(EC):
                exps_q(Half(1), c, fu)
            for t in range(NT):
                keys_values(Half(1), t, mu)
            hi_parts(x_hi_made, xt_hi, tu)
            act.wait_ge(prep, PREP_END)

            def half(h):
                tu, mu, fu = t_uses(h), m_uses(h), f_uses(h)
                near, late = h.n < NH - 2, h.n >= 1
                for t in range(NT):
                    tu.take()
                if h.n >= 2:
                    mu.take()
                if near:
                    exps_q(h.ahead(2), 0, fu)
                    keys_values(h.ahead(2), 0, mu)
                hi_parts(a_hi_made, at_hi, tu)
                for t in range(NT):
                    tu.take()
                if near:
                    keys_values(h.ahead(2), 1, mu)
                    exps_q(h.ahead(2), 1, fu)
                for t in range(NT):
                    mu.take()
                if near:
                    keys_values(h.ahead(2), 2, mu)
                    keys_values(h.ahead(2), 3, mu)
                hi_parts(h_hi_made, ht_hi, tu, scale="g1")
                if h.n == 0:
                    for _ in range(2):
                        tu.take()
                act.activation(table[:, 0:1], ones[:, 0:1], ACT.Gelu)
                for j in range(HC):
                    make_gelu(h, j, fu)
                    if j >= 1:
                        make_g_hi(h, j - 1)
                    if j == 3 and h.n < NH - 3:
                        hi_parts(x_hi_made, xt_hi, tu)
                make_g_hi(h, HC - 1)
                if h.n < NH - 3:
                    act.activation(table[:, 1:2], ones[:, 0:1], ACT.Exp)

            half(Half(0))
            half(Half(1))
            with act.Fori(0, LAPS) as lap:
                half(Half(2, lap))
                half(Half(3, lap))
            for n in PEELED:
                half(Half(n))

            a, b = Half(NH - 2), Half(NH - 1)
            tu, fu = t_uses(a), f_uses(a)

            def skip(n):
                for _ in range(n):
                    tu.take()

            skip(2 * NT)
            hi_parts(a_hi_made, at_hi, tu)
            skip(2)
            hi_parts(h_hi_made, ht_hi, tu, scale="g1")
            skip(2)
            for j in range(HC):
                make_gelu(a, j, fu)
                if j == 0:
                    hi_parts(a_hi_made, xt_hi, tu)
                if j >= 1:
                    make_g_hi(a, j - 1)
            make_g_hi(a, HC - 1)
            skip(NT)
            hi_parts(h_hi_made, ht_hi, tu, scale="g1")
            for j in range(HC):
                make_gelu(b, j, fu)
                if j >= 1:
                    make_g_hi(b, j - 1)
            make_g_hi(b, HC - 1)

            def rows_out(h, t, made):
                act.activation(y2[:, h.par, t], y2[:, h.par, t], ACT.Identity, scale=r3[:, t:t + 1],
                               bias=shift3[:, t:t + 1]).then_inc(made, 1)

            act.wait_ge(r3_made, a.at(3, 3))
            for t in range(NT):
                rows_out(a, t, out_made)
            act.wait_ge(r3_made, b.at(3, 3))
            for t in (2, 3):
                rows_out(b, t, last_out_made[1])

        @block.vector
        def _(dve):
            def lo_parts(sem_made, made, hi, lo, tu, scale=None):
                for c in range(EC):
                    u, bank = tu.take()
                    dve.wait_ge(sem_made, made + c + 1)
                    if scale is None:
                        ins = dve.tensor_tensor(lo[:, c], T[bank][:], f32(hi[:, c]), ALU.subtract)
                    else:
                        ins = dve.scalar_tensor_tensor(lo[:, c], T[bank][:], vcol(scale, c), f32(hi[:, c]),
                                                       ALU.mult, ALU.subtract)
                    ins.then_inc(t_drained, 1)

            def make_q(h, c, fu):
                _, bank = fu.take()
                dve.wait_ge(exp_q_made, h.at(EC, c + 1))
                dve.scalar_tensor_tensor(q_t[:, h.par, c], F[bank][:], bq_plus_1[:, c:c + 1], exp_q[:, c],
                                         ALU.add, ALU.max).then_inc(q_made, 1)

            def make_k(h, t, mu):
                _, bank = mu.take()
                dve.wait_ge(exp_k_made, h.at(NT, t + 1))
                dve.tensor_tensor(k_sb[:, t], exp_k[:, t % 2], M[bank][:, 0:E], ALU.max).then_inc(m_drained, 1)

            def carry_wait():
                dve.memset(unused[:, 3:4], 0.0)

            def make_kv(h):
                done = (h.n // 2) + h.lap
                dve.wait_ge(state_summed, done + 1)
                sums = state[:, 0:EC * AW].rearrange("p (c w) -> p c w", c=EC)
                dve.tensor_copy(k_sum[:], sums[:, :, P:P + 1]).then_inc(state_step, 1)
                dve.wait_ge(state_step, 3 * done + 1)
                for c in range(EC):
                    dve.scalar_tensor_tensor(kv_raw[:, c], bv_all[:, c * P:c * P + P], k_sum[:, c],
                                             state[:, c * AW:c * AW + P], ALU.mult, ALU.add).then_inc(state_step, 1)
                dve.wait_ge(state_step, 3 * done + 3)
                for c in range(EC):
                    dve.tensor_tensor(kv[:, c, 0:P], kv_raw[:, c], head_mask[:].rearrange("p h m -> p (h m)"),
                                      ALU.mult).then_inc(kv_made, 1)
                    dve.tensor_scalar(kv[:, c, P:AW], head_mask[:, :, 0], k_sum[:, c], None,
                                      ALU.mult).then_inc(kv_made, 1)

            def attn_sums(bank):
                return T[bank][:, 0:EC * AW].rearrange("p (c w) -> p c w", c=EC)

            def make_attn(h, tu, pair):
                tiles = [(t, *tu.take()) for t in (pair, pair + 1)]
                for t, u, bank in tiles:
                    dve.wait_ge(t_filled, u + 1)
                    dve.tensor_scalar(den[:, t].rearrange("p (c h) -> p c h", c=EC), attn_sums(bank)[:, :, P:AW],
                                      ATTN_EPS, None, ALU.add).then_inc(attn_step, 1)
                for i, (t, u, bank) in enumerate(tiles):
                    dve.wait_ge(attn_step, h.at(2 * NT, 2 * pair + 1 + i))
                    dve.reciprocal(inv_den[:, t], den[:, t]).then_inc(attn_step, 1)
                for i, (t, u, bank) in enumerate(tiles):
                    dve.wait_ge(attn_step, h.at(2 * NT, 2 * pair + 3 + i))
                    dve.tensor_tensor(attn[:, t].rearrange("p (c h m) -> p c h m", c=EC, h=HB),
                                      attn_sums(bank)[:, :, 0:P].rearrange("p c (h m) -> p c h m", h=HB),
                                      inv_den[:, t].rearrange("p (c h) -> p c h", c=EC)[:, :, :, None]
                                      .to_broadcast([P, EC, HB, HD]), ALU.mult).then_inc(t_drained, 1)

            def gelu_stats(part, t, tu):
                u, bank = tu.take()
                dve.wait_ge(t_filled, u + 1)
                dve.bn_stats(st2[:, t, part], T[bank][:]).then_inc(t_drained, 1)

            def gelu_moments(h, stats_drained):
                dve.wait_ge(t_drained, stats_drained)
                after(dve, r2_made, h.at(3, 0))
                carry_wait()
                for t in range(NT):
                    dve.bn_aggr(mv2[:, t], st2[:, t].rearrange("p a s -> p (a s)")).then_inc(ln2_step, 1)
                dve.wait_ge(ln2_step, h.at(NT + 2, NT))
                dve.tensor_scalar(var2[:], mv2[:, :, 1], LN_EPS, None, ALU.add).then_inc(ln2_step, 1)
                dve.tensor_scalar(minus_mean2[:], mv2[:, :, 0], -1.0, None, ALU.mult).then_inc(ln2_step, 1)

            def make_y1(h, mu):
                dve.wait_ge(x_bo_made, h.at(1, 1))
                after(dve, x1_made, h.at(NT, 0))
                for t in range(NT + 1):
                    if t < NT:
                        u, bank = mu.take()
                        dve.wait_ge(m_filled, u + 1)
                        dve.tensor_tensor(y1[:, t], M[bank][:, 0:E], x_bo[:, h.par, t], ALU.add).then_inc(m_drained, 1)
                    if t >= 1:
                        dve.wait_ge(m_drained, u if t < NT else u + 1)
                        dve.bn_stats(st1[:, t - 1], y1[:, t - 1]).then_inc(ln1_step, 1)
                dve.wait_ge(ln1_step, h.at(2 * NT + 2, NT))
                carry_wait()
                for t in range(NT):
                    dve.bn_aggr(mv1[:, t], st1[:, t]).then_inc(ln1_step, 1)
                dve.wait_ge(ln1_step, h.at(2 * NT + 2, 2 * NT))
                dve.tensor_scalar(var1[:, 0], mv1[:, :, 1], LN_EPS, None, ALU.add).then_inc(ln1_step, 1)
                dve.tensor_scalar(var1[:, 1], mv1[:, :, 1], 1.0 + LN_EPS, LN_EPS * LN_EPS, ALU.mult,
                                  ALU.add).then_inc(ln1_step, 1)

            def make_z(h):
                if h.n < NH - 2:
                    dve.wait_ge(q_made, h.ahead(2).at(EC, EC))
                dve.wait_ge(r1_made, h.at(4, 1))
                for t in range(NT):
                    dve.tensor_scalar(z[:, t], y1[:, t], mv1[:, t, 0:1], r1[:, 1, t:t + 1], ALU.subtract,
                                      ALU.mult).then_inc(z_made, 1)

            def make_y2(h, t, mu):
                u, bank = mu.take()
                if t == 0:
                    dve.wait_ge(out_free[h.par], 16 * (h.n // 2 + 1) + 16 * h.lap)
                dve.wait_ge(m_filled, u + 1)
                dve.wait_ge(x1_c_made, h.at(NT, t + 1))
                rows = F[t % 2] if in_f_bank(h, t) else M[bank]
                dve.scalar_tensor_tensor(y2[:, h.par, t], rows[:, 0:E], r2_step[:, t:t + 1], x1_e[:, h.par, t],
                                         ALU.mult, ALU.add).then_inc(m_drained, 1)

            def y2_stats(h, t):
                dve.bn_stats(st3[:, t], y2[:, h.par, t]).then_inc(ln3_step, 1)

            def y2_variance(h):
                after(dve, r3_made, h.at(3, 0))
                dve.wait_ge(ln3_step, h.at(2 * NT + 1, NT))
                carry_wait()
                for t in range(NT):
                    dve.bn_aggr(mv3[:, t], st3[:, t]).then_inc(ln3_step, 1)
                dve.wait_ge(ln3_step, h.at(2 * NT + 1, 2 * NT))
                dve.tensor_scalar(var3[:], mv3[:, :, 1], LN_EPS, None, ALU.add).then_inc(ln3_step, 1)

            def y2_moments(h, drained):
                dve.wait_ge(m_drained, drained)
                for t in range(NT):
                    y2_stats(h, t)
                y2_variance(h)

            def make_g_lo(h, j):
                dve.wait_ge(g_hi_made, h.at(HC, j + 1))
                dve.scalar_tensor_tensor(g_lo[:, h.par, j], g[:, j], vcol("g2", j), f32(g_hi[:, h.par, j]), ALU.mult,
                                         ALU.subtract).then_inc(g_lo_made, 1)

            steps = [0]

            def done(ins):
                steps[0] += 1
                ins.then_inc(prep, 1)

            def settled():
                dve.wait_ge(prep, steps[0])

            tu, mu, fu = Uses(0, 0, 3), Uses(0, 0, 2), Uses(0, 0, 2)

            def weight_lo(n, hi, lo):
                u, bank = tu.take()
                dve.wait_ge(w_hi_made, n)
                dve.tensor_tensor(lo, T[bank][:].rearrange("p (c e) -> p c e", c=EC), f32(hi),
                                  ALU.subtract).then_inc(t_drained, 1)

            dve.wait_ge(setup_made, 10)
            weight_lo(1, wq_hi[:], wq_lo[:])
            lo_parts(x_hi_made, 0, xt_hi, xt_lo, tu)
            weight_lo(2, wkv_hi[:, :, 0:E], wkv_lo[:, :, 0:E])
            weight_lo(3, wkv_hi[:, :, E:2 * E], wkv_lo[:, :, E:2 * E])
            u, bank = tu.take()
            dve.wait_ge(t_filled, u + 1)
            dve.tensor_copy(vec[:], T[bank][:, 0:NV]).then_inc(t_drained, 1)
            dve.wait_ge(t_drained, u + 1)
            done(dve.tensor_scalar(bq_plus_1[:], vec[:, 0:EC], 1.0, None, ALU.add))
            done(dve.tensor_scalar(minus_bq[:], vec[:, 0:EC], -1.0, None, ALU.mult))
            done(dve.tensor_copy(gc2[:, :, 0], vec[:, VEC["g2"][0]:VEC["g2"][0] + HC]))
            done(dve.tensor_copy(gc2[:, :, 1], vec[:, VEC["c2"][0]:VEC["c2"][0] + HC]))
            dve.wait_ge(rows_loaded, 64)
            done(dve.tensor_scalar(bk_row, bk_row, 1.0, None, ALU.add))
            assert steps[0] == PREP_VEC
            settled()
            done(dve.tensor_copy(bk_parts[:], bk_row))
            done(dve.tensor_scalar(bk_last[:], bk_row, ident[0:2, 1:2], None, ALU.mult))
            done(dve.tensor_tensor(row_sign[:], ident[0:2, 0:1], ident[0:2, 1:2], ALU.subtract))
            settled()
            done(dve.scalar_tensor_tensor(bk_parts[:], f32(bk_parts[:]), row_sign[:], bk_last[:], ALU.mult, ALU.add))
            assert steps[0] == PREP_BK

            def sum_abs(i, w, first, end):
                dve.wait_ge(ffn_loaded[i], 16)
                done(dve.tensor_reduce(abs_part[:, i, first:end],
                                       w.rearrange("p a (b e) -> p (a b) e", e=E)[:, first:end], AX.X, ALU.add,
                                       apply_absolute_value=True))

            def round_w(i, w):
                settled()
                done(dve.tensor_scalar(w, w, quant[:, i:i + 1], ROUND, ALU.mult, ALU.add))

            def clip_w(w):
                settled()
                done(dve.tensor_scalar(w, w, ROUND, 1.0, ALU.subtract, ALU.min))

            sum_abs(0, w1_raw, 0, HC)
            for c in range(EC):
                make_q(Half(0), c, fu)
            sum_abs(1, w2_raw, 0, HC // 2)
            make_k(Half(0), 0, mu)
            sum_abs(1, w2_raw, HC // 2, HC)
            make_k(Half(0), 1, mu)
            settled()
            done(dve.tensor_reduce(abs_sum[:], abs_part[:], AX.X, ALU.add))
            assert steps[0] == PREP_ABS
            make_k(Half(0), 2, mu)
            make_k(Half(0), 3, mu)
            u, bank = tu.take()
            dve.wait_ge(t_filled, u + 1)
            dve.tensor_scalar(mean_abs[:], T[bank][:, 0:2], 1.0 / (E * HID), SCALE_FLOOR, ALU.mult,
                              ALU.max).then_inc(t_drained, 1)
            dve.wait_ge(t_drained, u + 1)
            done(dve.reciprocal(quant[:], mean_abs[:]))
            settled()
            done(dve.reciprocal(step[:], quant[:]))
            lo_parts(x_hi_made, EC, xt_hi, xt_lo, tu)
            round_w(0, w1_raw)
            weight_lo(4, wo_hi[:], wo_lo[:])
            clip_w(w1_raw)
            assert steps[0] == PREP_TERN1

            def clip_w1(ec):
                for q in range(2):
                    u, bank = tu.take()
                    dve.wait_ge(t_filled, u + 1)
                    dve.tensor_scalar(w1_t[:, ec, q * 512:q * 512 + 512], T[bank][:], -1.0, None,
                                      ALU.max).then_inc(t_drained, 1)

            def clip_w2(q, tu):
                u, bank = tu.take()
                dve.wait_ge(t_filled, u + 1)
                dve.tensor_scalar(w2_t[:, 2 * q:2 * q + 2], T[bank][:].rearrange("p (i e) -> p i e", i=2), -1.0, None,
                                  ALU.max).then_inc(t_drained, 1)

            for c in range(EC):
                make_q(Half(1), c, fu)
            done(dve.tensor_copy(gc2_hi[:], gc2[:]))
            done(dve.tensor_copy(c1_parts[:, :, 0], vec[:, VEC["c1"][0]:VEC["c1"][0] + EC]))
            make_k(Half(1), 0, mu)
            clip_w1(0)
            round_w(1, w2_raw)
            make_k(Half(1), 1, mu)
            clip_w1(1)
            clip_w(w2_raw)
            make_k(Half(1), 2, mu)
            done(dve.tensor_tensor(gc2_lo[:], gc2[:], f32(gc2_hi[:]), ALU.subtract))
            done(dve.tensor_tensor(c1_parts[:, :, 1], vec[:, VEC["c1"][0]:VEC["c1"][0] + EC],
                                   f32(c1_parts[:, :, 0]), ALU.subtract))
            assert steps[0] == PREP_TERN2
            for i in range(2):
                done(dve.tensor_scalar(pick[:, i], ones[0:2, :], ident[0:2, i:i + 1], None, ALU.mult))
            for par in (0, 1):
                dve.memset(unused[:, par:par + 1], 0.0).then_inc(out_free[par], 16)
            make_k(Half(1), 3, mu)
            lo_parts(x_hi_made, 2 * EC, xt_hi, xt_lo, tu)
            u, bank = tu.take()
            dve.wait_ge(t_filled, u + 1)
            products = T[bank][:, 0:2 * HC].rearrange("p (j i) -> p j i", i=2)
            done(dve.scalar_tensor_tensor(b1_lo[:], products[:, :, 1], step[:, 0:1],
                                          vec[:, VEC["b1"][0]:VEC["b1"][0] + HC], ALU.mult, ALU.add))
            settled()
            dve.scalar_tensor_tensor(b1_all[:], products[:, :, 0], step[:, 0:1], b1_lo[:], ALU.mult,
                                     ALU.add).then_inc(t_drained, 1)
            dve.wait_ge(t_drained, u + 1)
            done(dve.memset(unused[:, 2:3], 0.0))
            assert steps[0] == PREP_END and tu.k == T_PRO
            make_kv(Half(1))

            def make_ce_rows(tu):
                u, bank = tu.take()
                dve.wait_ge(t_filled, u + 1)
                dve.tensor_copy(ce_rows[:], T[bank][0:2, 0:E]).then_inc(t_drained, 1)

            def make_ce(tu):
                u, bank = tu.take()
                dve.wait_ge(t_filled, u + 1)
                dve.tensor_copy(c_all[:], T[bank][:, 0:E]).then_inc(consts_made, 1)
                dve.scalar_tensor_tensor(e_all[:], T[bank][:, E:2 * E], step[:, 1:2], b2_all[:], ALU.mult,
                                         ALU.add).then_inc(consts_made, 1)
                dve.wait_ge(consts_made, 2)
                dve.memset(unused[:, 2:3], 0.0).then_inc(t_drained, 1)

            def half(h):
                tu, mu, fu = t_uses(h), m_uses(h), f_uses(h)
                near, late = h.n < NH - 2, h.n >= 1
                make_attn(h, tu, 0)
                if h.n >= 2:
                    make_y2(h.ahead(-2), NT - 1, mu)
                make_attn(h, tu, 2)
                if near:
                    make_q(h.ahead(2), 0, fu)
                    make_k(h.ahead(2), 0, mu)
                lo_parts(a_hi_made, h.at(EC), at_hi, at_lo, tu)
                if near:
                    make_k(h.ahead(2), 1, mu)
                if late:
                    gelu_stats(1, 0, tu)
                else:
                    clip_w2(0, tu)
                make_y1(h, mu)
                if near:
                    make_q(h.ahead(2), 1, fu)
                if late:
                    gelu_stats(1, 1, tu)
                else:
                    clip_w2(1, tu)
                make_z(h)
                for t in (2, 3):
                    if late:
                        gelu_stats(1, t, tu)
                    else:
                        clip_w2(t, tu)
                    if near:
                        make_k(h.ahead(2), t, mu)
                stats_drained = tu.first + tu.k
                lo_parts(h_hi_made, h.at(EC), ht_hi, ht_lo, tu, scale="g1")
                if h.n == 0:
                    make_ce_rows(tu)
                if late:
                    gelu_moments(h.ahead(-1), stats_drained)
                if h.n >= 2:
                    y2_moments(h.ahead(-2), mu.first + mu.k)
                if near and h.par == 1:
                    make_kv(h.ahead(2))
                for j in range(HC):
                    if late and j == 0:
                        make_y2(h.ahead(-1), 0, mu)
                    if j >= 4:
                        gelu_stats(0, j - 4, tu)
                    make_g_lo(h, j)
                    if h.n == 0 and j == 1:
                        make_ce(tu)
                    if late and j in FEED_2_AFTER:
                        t = 1 + FEED_2_AFTER.index(j)
                        make_y2(h.ahead(-1), t, mu)
                    if j == 2 and h.n < NH - 3:
                        lo_parts(x_hi_made, h.ahead(3).at(EC), xt_hi, xt_lo, tu)

            half(Half(0))
            half(Half(1))
            with dve.Fori(0, LAPS) as lap:
                half(Half(2, lap))
                half(Half(3, lap))
            for n in PEELED:
                half(Half(n))

            a, b = Half(NH - 2), Half(NH - 1)
            tu, mu = t_uses(a), m_uses(a)
            for t in range(NT):
                gelu_stats(1, t, tu)
            make_y2(a.ahead(-2), NT - 1, mu)
            gelu_moments(a.ahead(-1), tu.first + tu.k)
            make_attn(a, tu, 0)
            make_attn(a, tu, 2)
            make_y2(a.ahead(-1), 0, mu)
            lo_parts(a_hi_made, a.at(EC), at_hi, at_lo, tu)
            make_y2(a.ahead(-1), 1, mu)
            make_y2(a.ahead(-1), 2, mu)
            make_y1(a, mu)
            make_attn(b, tu, 0)
            make_z(a)
            make_y2(a.ahead(-1), 3, mu)
            lo_parts(h_hi_made, a.at(EC), ht_hi, ht_lo, tu, scale="g1")
            make_attn(b, tu, 2)
            y2_moments(a.ahead(-2), mu.first + mu.k)
            for j in range(HC):
                if j == 0:
                    lo_parts(a_hi_made, b.at(EC), xt_hi, xt_lo, tu)
                if j == 2:
                    make_y1(b, mu)
                if j >= 4:
                    gelu_stats(0, j - 4, tu)
                make_g_lo(a, j)
                if j == 4:
                    make_z(b)
            lo_parts(h_hi_made, b.at(EC), ht_hi, ht_lo, tu, scale="g1")
            for t in range(NT):
                gelu_stats(1, t, tu)
            gelu_moments(a, tu.first + tu.k)
            for j in range(HC):
                if j == 1:
                    y2_moments(a.ahead(-1), mu.first + mu.k)
                if 3 <= j <= 4:
                    make_y2(a, j - 3, mu)
                if j >= 4:
                    gelu_stats(0, j - 4, tu)
                make_g_lo(b, j)
            gelu_stats(1, 0, tu)
            make_y2(a, 2, mu)
            gelu_stats(1, 1, tu)
            gelu_stats(1, 2, tu)
            gelu_stats(1, 3, tu)
            make_y2(a, 3, mu)
            gelu_moments(b, tu.first + tu.k)
            y2_moments(a, mu.first + mu.k)
            dve.wait_ge(r2_made, b.at(3, 3))
            dve.wait_ge(x1_e_made, NH)
            for t in range(NT):
                dve.scalar_tensor_tensor(x1_e[:, b.par, t], c_all[:], shift2[:, t:t + 1], x1_e[:, b.par, t], ALU.mult,
                                         ALU.add).then_inc(x1_c_made, 1)
            for t in range(NT):
                make_y2(b, t, mu)
                if t == 1:
                    dve.wait_ge(ln3_step, b.at(2 * NT + 1, 0))
                if t >= 1:
                    dve.wait_ge(m_drained, mu.first + mu.k - 1)
                    y2_stats(b, t - 1)
            dve.wait_ge(m_drained, mu.first + mu.k)
            y2_stats(b, NT - 1)
            y2_variance(b)
            dve.wait_ge(r3_made, b.at(3, 1))
            for t in (0, 1):
                dve.tensor_scalar(y2[:, b.par, t], y2[:, b.par, t], mv3[:, t, 0:1], r3[:, t:t + 1], ALU.subtract,
                                  ALU.mult).then_inc(last_out_made[0], 1)


PREP_VEC = 5
PREP_BK = 9
PREP_ABS = 13
PREP_TERN1 = 17
PREP_TERN2 = 23
PREP_END = 27
X_TURNED = (3, 9)
ROUND = 1.5 * 2 ** 23
FEED_2_AFTER = (1, 3)
LAPS = 5
PEELED = (12, 13)

_INS = ['L0_attn_hidden_states', 'L0_attn_Wq', 'L0_attn_bq', 'L0_attn_Wk', 'L0_attn_bk', 'L0_attn_Wv', 'L0_attn_bv',
        'L0_attn_Wo', 'L0_attn_bo', 'L0_ffn_ln1_g', 'L0_ffn_ln1_b', 'L0_ffn_w1', 'L0_ffn_b1', 'L0_ffn_ln2_g',
        'L0_ffn_ln2_b', 'L0_ffn_w2', 'L0_ffn_b2']


def kernel(**inputs):
    import numpy as _np
    import concourse.bacc as _bacc
    from concourse import mybir as _mybir
    from concourse.bass_utils import run_bass_kernel_spmd as _run

    nc = _bacc.Bacc("TRN2", target_bir_lowering=False, num_devices=1)
    arrays, args = {}, []
    for name in _INS:
        a = _np.ascontiguousarray(inputs[name])
        arrays[f"in_{name}"] = a
        args.append(nc.dram_tensor(f"in_{name}", a.shape, _mybir.dt.from_np(a.dtype), kind="ExternalInput").ap())
    shape = inputs['L0_attn_hidden_states'].shape
    args.append(nc.dram_tensor("out_0", shape, _mybir.dt.float32, kind="ExternalOutput").ap())
    block_kernel(nc, *args)
    r = _run(nc, [arrays], core_ids=[0])
    return r.results[0]["out_0"]
```
